# Optimizing a Trainium2 kernel written in Bass

```python
import numpy as np
import jax
import jax.numpy as jnp

def _softmax(x, axis=-1):
    return jax.nn.softmax(x, axis=axis)

def _gelu(x):
    return jax.nn.gelu(x, approximate=True)

def _silu(x):
    return jax.nn.silu(x)

def _sigmoid(x):
    return jax.nn.sigmoid(x)

def _layernorm(x, axis=-1, eps=1e-05):
    m = jnp.mean(x, axis=axis, keepdims=True)
    v = jnp.var(x, axis=axis, keepdims=True)
    return (x - m) / jnp.sqrt(v + eps)

def _scatter_add(tgt, idx, src, axis=0):
    return tgt.at[idx].add(src)

def _segment_sum(src, seg, n):
    return jax.ops.segment_sum(src, seg, n)
kernel_name = 'mk_seq_postln_d1_jaxref_r8_6d6125'

def setup_inputs(seed: int=0):
    np.random.seed(seed)
    _w = jnp.asarray

    def _L0_attn_setup():
        import jax, jax.numpy as jnp
        import numpy as np
        DIM = 128
        N_HEADS = 16
        HEAD_DIM = DIM // N_HEADS
        B, T = (2, 256)
        ROPE_THETA = 32.0
        EPS = 1e-06

        def precompute_freqs_1d(dim, seq_len, theta):
            freqs = theta ** (-jnp.arange(0, dim, 2, dtype=jnp.float32) / dim)
            t = jnp.arange(seq_len, dtype=jnp.float32)
            ang = t[:, None] * freqs[None, :]
            return (jnp.cos(ang), jnp.sin(ang))

        def _rms_norm(t, w):
            var = jnp.mean(t * t, axis=-1, keepdims=True)
            return t * jax.lax.rsqrt(var + EPS) * w

        def _rope(q, k, cos, sin):
            cos = cos[None, None]
            sin = sin[None, None]
            q1, q2 = jnp.split(q, 2, axis=-1)
            k1, k2 = jnp.split(k, 2, axis=-1)
            q_out = jnp.concatenate([q1 * cos - q2 * sin, q2 * cos + q1 * sin], axis=-1)
            k_out = jnp.concatenate([k1 * cos - k2 * sin, k2 * cos + k1 * sin], axis=-1)
            return (q_out, k_out)
        key = jax.random.key(seed)
        k1, k2, k3, k4, k5 = jax.random.split(key, 5)
        x = jax.random.normal(k1, (B, T, DIM), dtype=jnp.float32)
        w_qkv = jax.random.normal(k2, (3 * DIM, DIM), dtype=jnp.float32) * DIM ** (-0.5)
        w_proj = jax.random.normal(k3, (DIM, DIM), dtype=jnp.float32) * DIM ** (-0.5)
        q_norm_w = 1.0 + 0.1 * jax.random.normal(k4, (HEAD_DIM,), dtype=jnp.float32)
        k_norm_w = 1.0 + 0.1 * jax.random.normal(k5, (HEAD_DIM,), dtype=jnp.float32)
        return {'x': x, 'w_qkv': w_qkv, 'w_proj': w_proj, 'q_norm_w': q_norm_w, 'k_norm_w': k_norm_w}
    _L0_attn_in = _L0_attn_setup()

    def _L0_ffn_setup():
        import jax, jax.numpy as jnp
        import numpy as np
        B, T, D = (2, 128, 128)
        H, DK, K = (8, 128, 8)
        NKEYS = 32
        NEXP = NKEYS * NKEYS

        def _rmsnorm(x, w, eps=1e-06):
            inv = jax.lax.rsqrt(jnp.mean(x * x, axis=-1, keepdims=True) + eps)
            return x * inv * w
        key = jax.random.key(seed)
        ks = jax.random.split(key, 5)
        return {'x': jax.random.normal(ks[0], (B, T, D), jnp.float32), 'w_q': jax.random.normal(ks[1], (H * 2 * DK, D), jnp.float32) * 0.02, 'keys': jax.random.normal(ks[2], (H, NKEYS, 2, DK), jnp.float32) * 0.02, 'expert_down': jax.random.normal(ks[3], (NEXP, D), jnp.float32) * 0.02, 'expert_up': jax.random.normal(ks[4], (NEXP, D), jnp.float32) * 0.02, 'norm_w': jnp.ones((D,), jnp.float32)}
    _L0_ffn_in = _L0_ffn_setup()
    _d = {'L0_attn_x': _L0_attn_in['x'], 'L0_attn_w_qkv': _L0_attn_in['w_qkv'], 'L0_attn_w_proj': _L0_attn_in['w_proj'], 'L0_attn_q_norm_w': _L0_attn_in['q_norm_w'], 'L0_attn_k_norm_w': _L0_attn_in['k_norm_w'], 'L0_ffn_w_q': _L0_ffn_in['w_q'], 'L0_ffn_keys': _L0_ffn_in['keys'], 'L0_ffn_expert_down': _L0_ffn_in['expert_down'], 'L0_ffn_expert_up': _L0_ffn_in['expert_up'], 'L0_ffn_norm_w': _L0_ffn_in['norm_w']}
    _x0 = _d['L0_attn_x']
    _d['L0_attn_x'] = jax.random.normal(jax.random.fold_in(jax.random.key(seed), 1), (16, 512, 128), dtype=_x0.dtype)
    del _x0
    return _d

def reference(L0_attn_x, L0_attn_w_qkv, L0_attn_w_proj, L0_attn_q_norm_w, L0_attn_k_norm_w, L0_ffn_w_q, L0_ffn_keys, L0_ffn_expert_down, L0_ffn_expert_up, L0_ffn_norm_w):

    def _L0_attn_ref(x, w_qkv, w_proj, q_norm_w, k_norm_w):
        import jax, jax.numpy as jnp
        import numpy as np
        DIM = 128
        N_HEADS = 16
        HEAD_DIM = DIM // N_HEADS
        B, T = (2, 256)
        ROPE_THETA = 32.0
        EPS = 1e-06

        def precompute_freqs_1d(dim, seq_len, theta):
            freqs = theta ** (-jnp.arange(0, dim, 2, dtype=jnp.float32) / dim)
            t = jnp.arange(seq_len, dtype=jnp.float32)
            ang = t[:, None] * freqs[None, :]
            return (jnp.cos(ang), jnp.sin(ang))

        def _rms_norm(t, w):
            var = jnp.mean(t * t, axis=-1, keepdims=True)
            return t * jax.lax.rsqrt(var + EPS) * w

        def _rope(q, k, cos, sin):
            cos = cos[None, None]
            sin = sin[None, None]
            q1, q2 = jnp.split(q, 2, axis=-1)
            k1, k2 = jnp.split(k, 2, axis=-1)
            q_out = jnp.concatenate([q1 * cos - q2 * sin, q2 * cos + q1 * sin], axis=-1)
            k_out = jnp.concatenate([k1 * cos - k2 * sin, k2 * cos + k1 * sin], axis=-1)
            return (q_out, k_out)
        Bc, Tc, C = x.shape
        scale = HEAD_DIM ** (-0.5)
        qkv = x @ w_qkv.T
        qkv = qkv.reshape(Bc, Tc, 3, N_HEADS, HEAD_DIM).transpose(2, 0, 3, 1, 4)
        q, k, v = (qkv[0], qkv[1], qkv[2])
        q = _rms_norm(q, q_norm_w)
        k = _rms_norm(k, k_norm_w)
        cos, sin = precompute_freqs_1d(HEAD_DIM, Tc, ROPE_THETA)
        q, k = _rope(q, k, cos, sin)
        attn = jnp.einsum('bhqd,bhkd->bhqk', q, k) * scale
        causal = jnp.triu(jnp.ones((Tc, Tc), dtype=bool), k=1)
        attn = jnp.where(causal, -jnp.inf, attn)
        attn = jax.nn.softmax(attn, axis=-1)
        out = jnp.einsum('bhqk,bhkd->bhqd', attn, v)
        out = out.transpose(0, 2, 1, 3).reshape(Bc, Tc, C)
        return out @ w_proj.T

    def _L0_ffn_ref(x, w_q, keys, expert_down, expert_up, norm_w):
        import jax, jax.numpy as jnp
        import numpy as np
        B, T, D = (2, 128, 128)
        H, DK, K = (8, 128, 8)
        NKEYS = 32
        NEXP = NKEYS * NKEYS

        def _rmsnorm(x, w, eps=1e-06):
            inv = jax.lax.rsqrt(jnp.mean(x * x, axis=-1, keepdims=True) + eps)
            return x * inv * w
        b, t, d = x.shape
        xn = _rmsnorm(x, norm_w)
        q = (xn @ w_q.T).reshape(b, t, H, 2, DK)
        sim1 = jnp.einsum('bthd,hkd->bthk', q[..., 0, :], keys[:, :, 0, :])
        sim2 = jnp.einsum('bthd,hkd->bthk', q[..., 1, :], keys[:, :, 1, :])
        s1, i1 = jax.lax.top_k(sim1, K)
        s2, i2 = jax.lax.top_k(sim2, K)
        all_idx = (i1[..., :, None] * NKEYS + i2[..., None, :]).reshape(b, t, H, K * K)
        all_sc = (s1[..., :, None] + s2[..., None, :]).reshape(b, t, H, K * K)
        fs, pk = jax.lax.top_k(all_sc, K)
        fi = jnp.take_along_axis(all_idx, pk, axis=-1)
        wd = expert_down[fi]
        wu = expert_up[fi]
        hidden = jax.nn.gelu(jnp.einsum('btd,bthkd->bthk', xn, wd), approximate=False)
        hidden = hidden * jax.nn.relu(fs)
        return jnp.einsum('bthk,bthkd->btd', hidden, wu)
    x = L0_attn_x
    x = _layernorm(x + _L0_attn_ref(x, L0_attn_w_qkv, L0_attn_w_proj, L0_attn_q_norm_w, L0_attn_k_norm_w), axis=-1)
    x = _layernorm(x + _L0_ffn_ref(x, L0_ffn_w_q, L0_ffn_keys, L0_ffn_expert_down, L0_ffn_expert_up, L0_ffn_norm_w), axis=-1)
    return x

_drawn_inputs = setup_inputs


def setup_inputs(seed=0):
    import zlib

    import numpy as np

    out = dict(_drawn_inputs(seed))
    spreads = {'L0_ffn_norm_w': (1.0, 0.6)}
    factors = {'L0_attn_q_norm_w': 4.07,
     'L0_attn_k_norm_w': 3.513,
     'L0_ffn_w_q': 8.0,
     'L0_ffn_keys': 8.0,
     'L0_ffn_expert_down': 8.0,
     'L0_ffn_expert_up': 8.0}
    for name, (base, spread) in spreads.items():
        noise = np.random.default_rng([zlib.crc32(name.encode()), seed]).standard_normal(out[name].shape)
        drawn = base * np.exp(spread * noise) if base else spread * noise
        out[name] = jnp.asarray(drawn.astype(out[name].dtype))
    for name, factor in factors.items():
        out[name] = (out[name] * factor).astype(out[name].dtype)
    return out
```

```python
import concourse.bass as bass
from concourse import mybir
from contextlib import ExitStack


class Signal:

    def __init__(self, sem, per_batch, seed=0):
        self.sem, self.per_batch, self.seed = sem, per_batch, seed

    def value(self, b, n):
        assert self.seed + n >= 1 or (isinstance(b, int) and b * self.per_batch + self.seed + n >= 1)
        return b * self.per_batch + (self.seed + n)


def attention_then_peer_layer(nc, x, w_qkv, w_proj, q_norm_w, k_norm_w, w_q, keys, expert_down, expert_up,
                              norm_w, rope_table, out):
    fp32, bf16, fp16, u16, u32 = (
        mybir.dt.float32, mybir.dt.bfloat16, mybir.dt.float16, mybir.dt.uint16, mybir.dt.uint32)
    ALU, ACT, AX = mybir.AluOpType, mybir.ActivationFunctionType, mybir.AxisListType

    P = 128
    BATCH, T, D = x.shape
    NT = T // P
    NH, HD = 16, 8
    NPAIR = NH // 2
    SLOTS = 8
    SCALE = float(HD) ** -0.5
    H, NK, TOPK = keys.shape[0], keys.shape[1], 8
    NEXP = expert_down.shape[0]
    NHI = NEXP // P
    NCAND = 20
    LN_EPS, RMS_EPS = 1e-5, 1e-6
    NEG = -1e30

    KC_AT = [0, 512, 1024, 896]
    PCOLS = 1280
    UNITS = 5 * 2
    NG = NH // 4

    ctx = ExitStack()
    with ctx:
        def sb(name, shape, dt):
            return ctx.enter_context(nc.sbuf_tensor(name, shape, dt))

        def pb(name):
            return ctx.enter_context(nc.psum_tensor(name, [P, 512], fp32))

        def sem(name):
            return ctx.enter_context(nc.semaphore(name))

        ident = sb("ident", [P, P], fp32)
        ident_b = sb("ident_b", [P, P], bf16)
        causal = sb("causal", [P, P], bf16)
        cand_no = sb("cand_no", [P, NCAND, TOPK], u16)
        minus_half = sb("minus_half", [P, 32], fp32)
        wqkvT = sb("wqkvT", [P, 3 * D], fp32)
        wprojT = sb("wprojT", [P, D], fp32)
        simW = sb("simW", [P, 2, H, NK], fp32)
        downT = sb("downT", [P, NEXP], fp32)
        up = sb("up", [P, NHI, D], fp32)
        normw = sb("normw", [P, 1], fp32)
        qkw = sb("qkw", [P, 2, HD], fp32)
        rope = sb("rope", [P, NT, 2, 4], fp32)
        cosw = sb("cosw", [P, NT, 2, HD], fp32)
        sinw = sb("sinw", [P, NT, 2, HD], fp32)
        xa = sb("xa", [P, NT, D], fp32)
        xr = sb("xr", [P, NT, D], fp32)
        xT = sb("xT", [P, T], fp32)
        qk_s = sb("qk_s", [P, 32, HD], fp32)
        qk_a = sb("qk_a", [P, 32, HD], fp32)
        qk_n = sb("qk_n", [P, 32, HD], fp32)
        qk_u = sb("qk_u", [P, 32, HD], fp32)
        qk_r = sb("qk_r", [P, 32, HD], fp32)
        qk_ms = sb("qk_ms", [P, 32], fp32)
        qk_rs = sb("qk_rs", [P, 32], fp32)
        stack = sb("stack", [P, 2, 2, NH, SLOTS, HD], bf16)
        qT = sb("qT", [P, NPAIR, T], bf16)
        kT = [sb("kT_even", [P, NPAIR, T], bf16), sb("kT_odd", [P, NPAIR, T], bf16)]
        vp = sb("vp", [P, NT, NH, HD + 1], fp32)
        prob = sb("prob", [P, 4, PCOLS], fp32)
        xn = sb("xn", [P, T], fp32)
        oT = xn
        rden = sb("rden", [P, NT, 4], fp32)
        o = sb("o", [P, NT, NH, HD], fp32)
        oTn = xT
        r1 = xr
        stats = sb("stats", [P, NT, 6], fp32)
        mv = sb("mv", [P, NT, 2], fp32)
        rs = sb("rs", [P, 5, NT], fp32)
        y = sb("y", [P, NT, D], fp32)
        yi = sb("yi", [P, NT, D], fp32)
        r2 = sb("r2", [P, NT, D], fp32)
        sims = sb("sims", [P, 2, 2, H, NK], fp32)
        topv = sb("topv", [P, NT, 2, H, TOPK], fp32)
        topi = sb("topi", [P, NT, 2, H, TOPK], u32)
        i12 = sb("i12", [P, 2, H, TOPK], fp32)
        candv = sb("candv", [P, 2, H, NCAND], fp32)
        cande = sb("cande", [P, 2, H, NCAND], fp16)
        fsel = sb("fsel", [P, NT, H, TOPK], fp32)
        psel = sb("psel", [P, 2, H, TOPK], u16)
        gat = sb("gat", [P, 2, H, NCAND, TOPK], fp16)
        esel = sb("esel", [P, NT, H * TOPK], fp32)
        eint = sb("eint", [P, 2, P], u16)
        elo = sb("elo", [P, 2, P], u16)
        ehi = sb("ehi", [P, 2, P], u16)
        wpart = sb("wpart", [P, 3, 2, P], bf16)
        wrest = sb("wrest", [P, 2, P], fp32)
        onehot = sb("onehot", [P, P, 2, P], bf16)
        hot_hi = sb("hot_hi", [P, NHI, 2 * P], bf16)
        whot = sb("whot", [P, 3, 2, NHI, P], bf16)
        hid = sb("hid", [P, NHI, T], fp32)

        tmp = onehot[:, :, :, :].rearrange("p a b c -> p (a b c)").bitcast(fp32)
        wq_raw = tmp[:, 0:2048].rearrange("p (g d) -> p g d", g=16)
        keys_raw = tmp[:, 2048:2560].rearrange("p (c s d) -> p c s d", c=2, s=2)
        keysT = tmp[:, 2560:3072]
        wqkv_raw = tmp[:, 3072:3456].rearrange("p (g d) -> p g d", g=3)
        wproj_raw = tmp[:, 3456:3584]
        down_raw = tmp[:, 3584:4608].rearrange("p (g d) -> p g d", g=8)

        S = [pb("S0"), pb("S1")]
        OV = pb("OV")
        A = pb("A")
        F = [pb("F0"), pb("F1")]
        G = [pb("G0"), pb("G1")]
        A_b = A[:, :].bitcast(bf16).rearrange("p (j t) -> p j t", j=NPAIR)

        w_loaded, const_done, zero_done = sem("w_loaded"), sem("const_done"), sem("zero_done")
        set_tr, set_ev, set_mm, set_w = sem("set_tr"), sem("set_ev"), sem("set_mm"), sem("set_w")

        waits_passed = sem("waits_passed")

        def signal(name, per_batch, seed=0):
            return Signal(sem(name), per_batch, seed)

        xa_loaded = signal("xa_loaded", 16)
        xr_loaded = signal("xr_loaded", 16)
        out_stored = signal("out_stored", 16, 16)
        a_ready = signal("a_ready", 19)
        xT_done = signal("xT_done", 1)
        sq_done = signal("sq_done", NT)
        ms_done = signal("ms_done", NT, 1)
        qrs_done = signal("qrs_done", 2 * NT)
        qn_done = signal("qn_done", NT)
        rope_done = signal("rope_done", 2 * NT, 2)
        rot_done = signal("rot_done", 2 * NT)
        first_done = signal("first_done", NT)
        rest_done = signal("rest_done", NT)
        second_done = signal("second_done", NT)
        stack_done = signal("stack_done", NT)
        v_done = signal("v_done", NT)
        qT_done = signal("qT_done", NT)
        kT_done = signal("kT_done", NT)
        s_ready = signal("s_ready", NG * UNITS)
        exp_done = signal("exp_done", NG * UNITS, 2)
        pv_done = signal("pv_done", NG, 1)
        oT_done = signal("oT_done", NG, 1)
        rden_done = signal("rden_done", NG)
        o_done = signal("o_done", NG)
        oTn_done = signal("oTn_done", 1)
        ln1 = signal("ln1", 11, 11)
        yi_done = signal("yi_done", 1)
        f_ready = signal("f_ready", 16)
        xn_done = signal("xn_done", 1)
        sims_done = signal("sims_done", NT)
        topv_done = signal("topv_done", NT)
        top1_done = signal("top1_done", NT, 2)
        i12_done = signal("i12_done", NT)
        cand_done = signal("cand_done", NT, 1)
        fsel_done = signal("fsel_done", NT)
        top2_done = signal("top2_done", NT)
        hotc_done = signal("hotc_done", NT)
        gat_done = signal("gat_done", 2 * NT)
        esel_done = signal("esel_done", NT)
        hid_done = signal("hid_done", NHI)
        dec = signal("dec", 8, 8)
        hot_done = signal("hot_done", 3)
        g_ready = signal("g_ready", 8)
        g_free = signal("g_free", 8, 2)
        r2_done = signal("r2_done", 1)
        ln2 = signal("ln2", 5, 5)
        out_ready = signal("out_ready", 1)
        seeded = [out_stored, ms_done, rope_done, exp_done, pv_done, oT_done, ln1, dec, ln2, cand_done, top1_done, g_free]

        A_USES = [("xT", [(xT_done, 1)]), ("qkv0", [(v_done, 1), (qn_done, 1)])]
        for t in range(NT):
            if t + 1 < NT:
                A_USES.append((f"qkv{t + 1}", [(v_done, t + 2), (qn_done, t + 2)]))
            A_USES += [(f"Q{t}", [(qT_done, t + 1)]), (f"K{t}", [(kT_done, t + 1)])]
        A_USES += [(f"o{g}", [(o_done, g + 1)]) for g in range(NG)]
        A_USES += [("oTn", [(oTn_done, 1)]), ("proj", [(ln1, 1)])]
        F_USES = [("xn", [(xn_done, 1)])]
        F_USES += [(f"sims{t}", [(sims_done, t + 1)]) for t in (0, 1)]
        F_USES += [(f"hid{c}", [(hid_done, c + 1)]) for c in range(NHI)]
        F_USES += [(f"sims{t}", [(sims_done, t + 1)]) for t in (2, 3)]
        F_USES += [("sel0", [(dec, 2)]), ("sel1", [(dec, 6)]), ("ffn", [(ln2, 1)])]

        def pass_wait(eng):
            eng.sem_inc(waits_passed, 1)

        def number(uses, use):
            return [name for name, _ in uses].index(use)

        def wait_read(eng, b, uses, i):
            for s, n in uses[i][1]:
                eng.wait_ge(s.sem, s.value(b, n - s.per_batch if i < 0 else n))

        def a_filled(b, use):
            return a_ready.value(b, number(A_USES, use) + 1)

        def wait_a_empty(eng, b, use):
            wait_read(eng, b, A_USES, number(A_USES, use) - 1)

        def bank_f(use):
            return F[number(F_USES, use) % 2]

        def f_filled(b, use):
            return f_ready.value(b, number(F_USES, use) + 1)

        def wait_f_empty(eng, b, use):
            wait_read(eng, b, F_USES, number(F_USES, use) - 2)

        SCORES = [[(0, 0, 0)], [(0, 1, 0), (0, 3, 384)], [(0, 2, 0), (1, 2, 256)],
                  [(1, 0, 0)], [(1, 1, 0), (1, 3, 384)]]

        block = ctx.enter_context(nc.Block())

        @block.sync
        def _(sp):
            loads = [
                (wq_raw, w_q.rearrange("(g p) d -> p g d", p=P)),
                (keys_raw, keys.rearrange("(c h) k s d -> (h k) c s d", c=2)),
                (wqkv_raw, w_qkv.rearrange("(g p) d -> p g d", p=P)),
                (wproj_raw, w_proj),
                (down_raw, expert_down.rearrange("(g p) d -> p g d", p=P)),
                (up[:, :, :], expert_up.rearrange("(g p) d -> p g d", p=P)),
                (normw[:, :], norm_w.rearrange("(p a) -> p a", a=1)),
                (qkw[:, 0, :], q_norm_w.rearrange("(a n) -> a n", a=1).to_broadcast([P, HD])),
                (qkw[:, 1, :], k_norm_w.rearrange("(a n) -> a n", a=1).to_broadcast([P, HD])),
                (rope[:, :, :, :], rope_table.rearrange("(t p) c d -> p t c d", p=P)),
            ]
            for dst, src in loads:
                sp.dma_start(dst, src).then_inc(w_loaded, 16)

            def load_xa(b):
                sp.dma_start(xa[:, :, :], x[b].rearrange("(t p) d -> p t d", p=P)).then_inc(xa_loaded.sem, 16)

            def load_xr(b):
                sp.dma_start(xr[:, :, :], x[b].rearrange("(t p) d -> p t d", p=P)).then_inc(xr_loaded.sem, 16)

            def store(b):
                sp.wait_ge(out_ready.sem, out_ready.value(b, 1))
                sp.dma_start(out[b].rearrange("(t p) d -> p t d", p=P), r2[:, :, :]).then_inc(out_stored.sem, 16)

            def next_xa(b):
                sp.wait_ge(a_ready.sem, a_filled(b, "xT"))
                load_xa(b + 1)

            def next_xr(b):
                sp.wait_ge(ln1.sem, ln1.value(b, 11))
                load_xr(b + 1)

            load_xa(0)
            load_xr(0)
            next_xa(0)
            next_xr(0)
            with sp.Fori(1, BATCH - 1) as b:
                next_xa(b)
                store(b - 1)
                next_xr(b)
            store(BATCH - 2)
            store(BATCH - 1)
            sp.wait_ge(out_stored.sem, out_stored.value(BATCH - 1, 16))

        @block.gpsimd
        def _(pool):
            pool.memset(ident[:, :], 0.0).then_inc(zero_done, 1)
            pool.memset(ident_b[:, :], 0.0).then_inc(zero_done, 1)
            pool.memset(minus_half[:, :], -0.5)
            pool.memset(causal[:, :], 0.0).then_inc(zero_done, 1)
            pool.wait_ge(zero_done, 3)
            for m in (ident, ident_b):
                pool.affine_select(out=m[:, :], in_=m[:, :], compare_op=ALU.not_equal, fill=1.0, base=0,
                                   pattern=[[-1, P]], channel_multiplier=1).then_inc(const_done, 1)
            pool.affine_select(out=causal[:, :], in_=causal[:, :], compare_op=ALU.is_ge, fill=NEG, base=0,
                               pattern=[[1, P]], channel_multiplier=-1).then_inc(const_done, 1)
            pool.iota(cand_no[:, :, :], pattern=[[1, NCAND], [0, TOPK]], base=0, channel_multiplier=0).then_inc(const_done, 1)
            pool.wait_ge(const_done, 4)

            def roots(b, t):
                pool.wait_ge(ms_done.sem, ms_done.value(b, t + 1))
                pass_wait(pool)
                pool.tensor_scalar(qk_rs[:, :], qk_ms[:, :], HD * RMS_EPS, None, ALU.add).then_inc(qrs_done.sem, 1)
                pool.wait_ge(qrs_done.sem, qrs_done.value(b, 2 * t + 1))
                pool.tensor_tensor(qk_rs[:, :], qk_rs[:, :], minus_half[:, :], ALU.pow).then_inc(qrs_done.sem, 1)

            def deviations(b, signal, n):
                pool.wait_ge(signal.sem, signal.value(b, n))
                pass_wait(pool)
                pool.tensor_scalar(rs[:, 1, :], mv[:, :, 1], LN_EPS, None, ALU.add).then_inc(signal.sem, 1)
                pool.wait_ge(signal.sem, signal.value(b, n + 1))
                pool.tensor_tensor(rs[:, 0, :], rs[:, 1, :], minus_half[:, 0:NT], ALU.pow).then_inc(signal.sem, 1)
                pool.wait_ge(signal.sem, signal.value(b, n + 2))

            def root_mean_squares(b):
                deviations(b, ln1, 3)
                pool.tensor_tensor(rs[:, 1, :], mv[:, :, 1], rs[:, 0, :], ALU.mult).then_inc(ln1.sem, 1)
                pool.wait_ge(ln1.sem, ln1.value(b, 6))
                pool.tensor_tensor(rs[:, 2, :], rs[:, 1, :], rs[:, 0, :], ALU.mult).then_inc(ln1.sem, 1)
                pool.wait_ge(ln1.sem, ln1.value(b, 7))
                pass_wait(pool)
                pool.tensor_scalar(rs[:, 1, :], rs[:, 2, :], RMS_EPS, None, ALU.add).then_inc(ln1.sem, 1)
                pool.wait_ge(ln1.sem, ln1.value(b, 8))
                pool.tensor_tensor(rs[:, 3, :], rs[:, 1, :], minus_half[:, 0:NT], ALU.pow).then_inc(ln1.sem, 1)
                pool.wait_ge(ln1.sem, ln1.value(b, 9))
                pool.tensor_tensor(rs[:, 4, :], rs[:, 3, :], rs[:, 0, :], ALU.mult).then_inc(ln1.sem, 1)

            def rotate(b, t):
                pool.wait_ge(qn_done.sem, qn_done.value(b, t + 1))
                by_side = lambda a: a[:, :, :].rearrange("p (s h) d -> p s h d", s=2)
                for dst, tab in ((qk_a, cosw), (qk_u, sinw)):
                    w = tab[:, t, :, :].unsqueeze(2).to_broadcast([P, 2, NH, HD])
                    pool.tensor_tensor(by_side(dst), by_side(qk_n), w, ALU.mult).then_inc(rope_done.sem, 1)
                pool.wait_ge(rope_done.sem, rope_done.value(b, 2 * t + 2))
                pool.tensor_tensor(qk_r[:, :, 0:4], qk_a[:, :, 0:4], qk_u[:, :, 4:8], ALU.subtract)\
                    .then_inc(rot_done.sem, 1)
                pool.tensor_tensor(qk_r[:, :, 4:8], qk_a[:, :, 4:8], qk_u[:, :, 0:4], ALU.add)\
                    .then_inc(rot_done.sem, 1)

            def split(b, t):
                st = stack[:, t % 2]
                r = qk_r[:, :, :].rearrange("p (s h) d -> p s h d", s=2)
                u = qk_u[:, :, :].rearrange("p (s h) d -> p s h d", s=2)
                pool.wait_ge(first_done.sem, first_done.value(b, t + 1))
                pool.tensor_tensor(u, r, st[:, :, :, 2, :], ALU.subtract).then_inc(rest_done.sem, 1)
                pool.wait_ge(second_done.sem, second_done.value(b, t + 1))
                pool.tensor_tensor(st[:, 0, :, 4, :], u[:, 0], st[:, 0, :, 5, :], ALU.subtract)
                pool.tensor_tensor(st[:, 1, :, 0, :], u[:, 1], st[:, 1, :, 5, :], ALU.subtract)\
                    .then_inc(stack_done.sem, 1)

            def candidates(b, t):
                pool.wait_ge(top1_done.sem, top1_done.value(b, t + 1))
                pool.wait_ge(cand_done.sem, cand_done.value(b, t))
                pass_wait(pool)
                for side, scale in enumerate((NK, 1)):
                    last = pool.tensor_scalar(i12[:, side], topi[:, t, side], float(scale), None, ALU.mult)
                last.then_inc(i12_done.sem, 1)
                pool.wait_ge(i12_done.sem, i12_done.value(b, t + 1))
                last = None
                for dst, one, two in ((candv, topv[:, t, 0], topv[:, t, 1]), (cande, i12[:, 0], i12[:, 1])):
                    c = dst[:, t % 2]
                    pool.tensor_tensor(c[:, :, 0:8], one[:, :, 0:1].to_broadcast([P, H, 8]), two, ALU.add)
                    pool.tensor_tensor(c[:, :, 8:12], one[:, :, 1:2].to_broadcast([P, H, 4]), two[:, :, 0:4],
                                       ALU.add)
                    pool.tensor_tensor(c[:, :, 12:16].rearrange("p h (a b) -> p h a b", a=2),
                                       one[:, :, 2:4].unsqueeze(3).to_broadcast([P, H, 2, 2]),
                                       two[:, :, 0:2].unsqueeze(2).to_broadcast([P, H, 2, 2]), ALU.add)
                    last = pool.tensor_tensor(c[:, :, 16:20], one[:, :, 4:8],
                                              two[:, :, 0:1].to_broadcast([P, H, 4]), ALU.add)
                last.then_inc(cand_done.sem, 1)

            def gather(b, t):
                pool.wait_ge(hotc_done.sem, hotc_done.value(b, t + 1))
                g = gat[:, t % 2]
                pool.tensor_tensor(g, g, cande[:, t % 2].unsqueeze(3).to_broadcast([P, H, NCAND, TOPK]), ALU.mult)\
                    .then_inc(gat_done.sem, 1)
                pool.wait_ge(gat_done.sem, gat_done.value(b, 2 * t + 1))
                pool.tensor_tensor(g[:, :, 0:10], g[:, :, 0:10], g[:, :, 10:20], ALU.add)\
                    .then_inc(gat_done.sem, 1)

            def batch(b, f):
                for t in range(NT):
                    if b is not None:
                        roots(b, t)
                        rotate(b, t)
                        split(b, t)
                    if f is not None:
                        candidates(f, t)
                        if t >= 1:
                            gather(f, t - 1)
                if f is not None:
                    gather(f, NT - 1)
                    deviations(f, ln2, 3)
                if b is not None:
                    root_mean_squares(b)

            batch(0, None)
            with pool.Fori(1, BATCH) as b:
                batch(b, b - 1)
            batch(None, BATCH - 1)

        @block.scalar
        def _(act):
            act.wait_ge(w_loaded, 160)

            def normed(b):
                act.wait_ge(f_ready.sem, f_filled(b, "xn"))
                bank = bank_f("xn")
                act.activation(xn[:, :], bank[:, :], ACT.Copy, scale=normw[:, 0:1]).then_inc(xn_done.sem, 1)

            def similarities(b, t):
                act.wait_ge(f_ready.sem, f_filled(b, f"sims{t}"))
                act.wait_ge(top1_done.sem, top1_done.value(b, t - 1))
                bank = bank_f(f"sims{t}")
                act.activation(sims[:, t % 2].rearrange("p s h k -> p (s h k)"), bank[:, :], ACT.Copy)\
                    .then_inc(sims_done.sem, 1)

            def hidden(b, c):
                act.wait_ge(f_ready.sem, f_filled(b, f"hid{c}"))
                bank = bank_f(f"hid{c}")
                act.activation(hid[:, c, :], bank[:, :], ACT.Gelu).then_inc(hid_done.sem, 1)

            def squares(b, t):
                act.wait_ge(a_ready.sem, a_filled(b, f"qkv{t}"))
                act.wait_ge(ms_done.sem, ms_done.value(b, t))
                act.activation(qk_s[:, :, :].rearrange("p g d -> p (g d)"), A[:, 0:2 * D], ACT.Square)\
                    .then_inc(sq_done.sem, 1)
                act.activation(vp[:, t, :, 0:HD], A[:, 2 * D:3 * D].rearrange("p (h d) -> p h d", h=NH), ACT.Copy)\
                    .then_inc(v_done.sem, 1)

            def parts(b, t):
                st = stack[:, t % 2]
                r = qk_r[:, :, :].rearrange("p (s h) d -> p s h d", s=2)
                u = qk_u[:, :, :].rearrange("p (s h) d -> p s h d", s=2)
                act.wait_ge(rot_done.sem, rot_done.value(b, 2 * t + 2))
                three = [P, NH, 3, HD]
                act.activation(st[:, 0, :, 0:3, :], r[:, 0].unsqueeze(2).to_broadcast(three), ACT.Copy)
                act.activation(st[:, 1, :, 2:5, :], r[:, 1].unsqueeze(2).to_broadcast(three), ACT.Copy)\
                    .then_inc(first_done.sem, 1)
                act.wait_ge(rest_done.sem, rest_done.value(b, t + 1))
                two = [P, NH, 2, HD]
                act.activation(st[:, 0, :, 3:6:2, :], u[:, 0].unsqueeze(2).to_broadcast(two), ACT.Copy)
                act.activation(st[:, 1, :, 1:6:4, :], u[:, 1].unsqueeze(2).to_broadcast(two), ACT.Copy)\
                    .then_inc(second_done.sem, 1)

            def transposed(b, t):
                act.wait_ge(a_ready.sem, a_filled(b, f"Q{t}"))
                act.activation(qT[:, :, t * P:(t + 1) * P], A_b, ACT.Copy).then_inc(qT_done.sem, 1)
                act.wait_ge(a_ready.sem, a_filled(b, f"K{t}"))
                act.activation(kT[0][0:64, :, t * P:(t + 1) * P], A_b[0:64], ACT.Copy)
                act.activation(kT[1][64:128, :, t * P:(t + 1) * P], A_b[64:128], ACT.Copy).then_inc(kT_done.sem, 1)

            def exps(b, g):
                act.wait_ge(pv_done.sem, pv_done.value(b, g))
                for u in range(UNITS):
                    n = g * UNITS + u
                    act.wait_ge(s_ready.sem, s_ready.value(b, n + 1))
                    h = 2 * (u // 5)
                    src = S[n % 2][:, :]
                    if u % 5 == 2:
                        dst = prob[:, h:h + 2, KC_AT[2]:KC_AT[2] + 256]
                        src = src.rearrange("p (h n) -> p h n", h=2)
                    else:
                        h, at = (h + u % 5 // 3, 0 if u % 5 in (0, 3) else 512)
                        dst = prob[:, h, at:at + 512]
                    act.activation(dst, src, ACT.Exp, scale=SCALE).then_inc(exp_done.sem, 1)

            def attended(b, g):
                act.wait_ge(pv_done.sem, pv_done.value(b, g + 1))
                if g:
                    act.wait_ge(a_ready.sem, a_filled(b, f"o{g - 1}"))
                act.activation(oT[:, :], OV[:, :], ACT.Copy).then_inc(oT_done.sem, 1)

            def batch(b, f):
                if f is not None:
                    normed(f)
                    similarities(f, 0)
                    similarities(f, 1)
                    for c in range(NHI):
                        hidden(f, c)
                    similarities(f, 2)
                    similarities(f, 3)
                if b is not None:
                    act.wait_ge(a_ready.sem, a_filled(b, "xT"))
                    act.activation(xT[:, :], A[:, :], ACT.Copy).then_inc(xT_done.sem, 1)
                    squares(b, 0)
                    parts(b, 0)
                    for t in range(NT):
                        if t + 1 < NT:
                            squares(b, t + 1)
                        transposed(b, t)
                        if t + 1 < NT:
                            parts(b, t + 1)
                    for g in range(NG):
                        exps(b, g)
                        attended(b, g)
                    act.wait_ge(a_ready.sem, a_filled(b, "oTn"))
                    act.activation(oTn[:, :], A[:, :], ACT.Copy).then_inc(oTn_done.sem, 1)

            batch(0, None)
            with act.Fori(1, BATCH) as b:
                batch(b, b - 1)
            batch(None, BATCH - 1)

        @block.tensor
        def _(pe):
            pe.wait_ge(w_loaded, 160)
            pe.wait_ge(const_done, 4)
            raw = ([wqkv_raw[:, g, :] for g in range(3)] + [wproj_raw] + [down_raw[:, g, :] for g in range(8)]
                   + [keys_raw[:, c, s, :] for s in range(2) for c in range(2)])
            for bank, quad in zip((S[0], S[1], OV, A), range(4)):
                for i in range(4):
                    last = nc.tensor.transpose(bank[:, i * P:(i + 1) * P], raw[4 * quad + i], ident[:, :])
                last.then_inc(set_tr, 1)
            pe.wait_ge(set_ev, 4)
            for s in range(2):
                for h in range(H):
                    col = (s * H + h) * NK
                    last = nc.tensor.matmul(G[0][:, col:col + NK], wq_raw[:, 2 * h + s, :],
                                            keysT[:, col:col + NK], start=True, stop=True)
            last.then_inc(set_mm, 1)
            pe.wait_ge(set_w, 1)

            def transpose_x(b):
                pe.wait_ge(xa_loaded.sem, xa_loaded.value(b, 16))
                wait_a_empty(pe, b, "xT")
                for t in range(NT):
                    last = nc.tensor.transpose(A[:, t * P:(t + 1) * P], xa[:, t, :], ident[:, :])
                last.then_inc(a_ready.sem, 1)

            def project_qkv(b, t):
                if t == 0:
                    pe.wait_ge(xT_done.sem, xT_done.value(b, 1))
                wait_a_empty(pe, b, f"qkv{t}")
                nc.tensor.matmul(A[:, 0:3 * D], xT[:, t * P:(t + 1) * P], wqkvT[:, :], start=True, stop=True)\
                    .then_inc(a_ready.sem, 1)

            def transpose_stack(b, t):
                pe.wait_ge(stack_done.sem, stack_done.value(b, t + 1))
                for side, use in enumerate("QK"):
                    wait_a_empty(pe, b, f"{use}{t}")
                    st = stack[:, t % 2, side].rearrange("p (j h) s d -> p j (h s d)", h=2)
                    for j in range(NPAIR):
                        last = nc.tensor.transpose(A_b[:, j, :], st[:, j, :], ident_b[:, :])
                    last.then_inc(a_ready.sem, 1)

            def scores(b, g, units):
                if g == 0:
                    pe.wait_ge(kT_done.sem, kT_done.value(b, NT))
                for u in units:
                    n = g * UNITS + u
                    pe.wait_ge(exp_done.sem, exp_done.value(b, n - 1))
                    j = 2 * g + u // 5
                    bank = S[n % 2]
                    for half, kc, col in SCORES[u % 5]:
                        pe_k = kT[half][:, j, kc * P:(kc + 1) * P]
                        nc.tensor.matmul(bank[:, col:col + T - kc * P], pe_k, qT[:, j, kc * P:T],
                                         start=True, stop=False, skip_group_check=True)
                        last = nc.tensor.matmul(bank[:, col:col + P], ident_b[:, :], causal[:, :],
                                                start=False, stop=True, skip_group_check=True)
                    last.then_inc(s_ready.sem, 1)

            def attend(b, g):
                pe.wait_ge(exp_done.sem, exp_done.value(b, (g + 1) * UNITS))
                pe.wait_ge(oT_done.sem, oT_done.value(b, g))
                for kc in range(NT):
                    for i in range(4):
                        last = nc.tensor.matmul(
                            OV[32 * i:32 * i + HD + 1, kc * P:T], vp[:, kc, 4 * g + i, :],
                            prob[:, i, KC_AT[kc]:KC_AT[kc] + T - kc * P], start=(kc == 0), stop=(kc == NT - 1),
                            skip_group_check=True)
                last.then_inc(pv_done.sem, 1)

            def transpose_o(b, g):
                pe.wait_ge(oT_done.sem, oT_done.value(b, g + 1))
                wait_a_empty(pe, b, f"o{g}")
                for t in range(NT):
                    last = nc.tensor.transpose(A[:, t * P:(t + 1) * P], oT[:, t * P:(t + 1) * P], ident[:, :])
                last.then_inc(a_ready.sem, 1)

            def project_out(b):
                pe.wait_ge(o_done.sem, o_done.value(b, NG))
                wait_a_empty(pe, b, "oTn")
                for t in range(NT):
                    last = nc.tensor.transpose(A[:, t * P:(t + 1) * P],
                                               o[:, t].rearrange("p h d -> p (h d)"), ident[:, :])
                last.then_inc(a_ready.sem, 1)
                pe.wait_ge(oTn_done.sem, oTn_done.value(b, 1))
                wait_a_empty(pe, b, "proj")
                for t in range(NT):
                    last = nc.tensor.matmul(A[:, t * P:(t + 1) * P], oTn[:, t * P:(t + 1) * P], wprojT[:, :],
                                            start=True, stop=True)
                last.then_inc(a_ready.sem, 1)

            def project_similarities(b, t):
                bank = bank_f(f"sims{t}")
                wait_f_empty(pe, b, f"sims{t}")
                nc.tensor.matmul(bank[:, :], xn[:, t * P:(t + 1) * P],
                                 simW[:, :, :, :].rearrange("p s h k -> p (s h k)"), start=True, stop=True)\
                    .then_inc(f_ready.sem, 1)

            def ffn_head(b):
                bank = bank_f("xn")
                pe.wait_ge(yi_done.sem, yi_done.value(b, 1))
                wait_f_empty(pe, b, "xn")
                for t in range(NT):
                    last = nc.tensor.transpose(bank[:, t * P:(t + 1) * P], yi[:, t, :], ident[:, :])
                last.then_inc(f_ready.sem, 1)
                pe.wait_ge(xn_done.sem, xn_done.value(b, 1))
                project_similarities(b, 0)
                project_similarities(b, 1)
                for c in range(NHI):
                    bank = bank_f(f"hid{c}")
                    wait_f_empty(pe, b, f"hid{c}")
                    nc.tensor.matmul(bank[:, :], downT[:, c * P:(c + 1) * P], xn[:, :], start=True, stop=True)\
                        .then_inc(f_ready.sem, 1)
                project_similarities(b, 2)
                project_similarities(b, 3)

            def transpose_selection(b, pair):
                bank = bank_f(f"sel{pair}")
                pe.wait_ge(esel_done.sem, esel_done.value(b, 2 * pair + 2))
                wait_f_empty(pe, b, f"sel{pair}")
                nc.tensor.transpose(bank[:, 0:P], esel[:, 2 * pair:2 * pair + 2, :].rearrange("p t k -> p (t k)"),
                                    ident[:, :])
                nc.tensor.transpose(bank[:, P:2 * P], fsel[:, 2 * pair:2 * pair + 2].rearrange("p t h k -> p (t h k)"),
                                    ident[:, :]).then_inc(f_ready.sem, 1)

            def weights(b, chunk):
                if chunk % 4 == 0:
                    pe.wait_ge(hot_done.sem, hot_done.value(b, 2 + chunk // 4))
                pe.wait_ge(g_free.sem, g_free.value(b, chunk - 1))
                pair, bank = chunk // 4, G[chunk % 2]
                for i in range(32):
                    t = chunk % 4 * 32 + i
                    for part in range(3):
                        last = nc.tensor.matmul(bank[:, 16 * i:16 * i + 16], onehot[:, :, pair, t],
                                                whot[:, part, :, :, t],
                                                start=(part == 0), stop=(part == 2))
                last.then_inc(g_ready.sem, 1)

            def expert_outputs(b):
                bank = bank_f("ffn")
                pe.wait_ge(g_free.sem, g_free.value(b, 8))
                wait_f_empty(pe, b, "ffn")
                for t in range(NT):
                    for c in range(NHI):
                        last = nc.tensor.matmul(bank[:, t * P:(t + 1) * P], hid[:, c, t * P:(t + 1) * P],
                                                up[:, c, :], start=(c == 0), stop=(c == NHI - 1))
                last.then_inc(f_ready.sem, 1)

            def batch(b, f):
                if f is not None:
                    ffn_head(f)
                if b is not None:
                    transpose_x(b)
                    project_qkv(b, 0)
                    for t in range(NT):
                        if t + 1 < NT:
                            project_qkv(b, t + 1)
                        transpose_stack(b, t)
                for g in range(NG):
                    if b is not None:
                        scores(b, g, range(0, 2))
                        if g:
                            attend(b, g - 1)
                        scores(b, g, range(2, UNITS))
                        if g:
                            transpose_o(b, g - 1)
                    if f is not None and g == 1:
                        transpose_selection(f, 0)
                        transpose_selection(f, 1)
                    if f is not None and g >= 2:
                        weights(f, 2 * g - 4)
                        weights(f, 2 * g - 3)
                if b is not None:
                    attend(b, NG - 1)
                    transpose_o(b, NG - 1)
                if f is not None:
                    for chunk in range(4, 8):
                        weights(f, chunk)
                    expert_outputs(f)
                if b is not None:
                    project_out(b)

            batch(0, None)
            with pe.Fori(1, BATCH) as b:
                batch(b, b - 1)
            batch(None, BATCH - 1)

        @block.vector
        def _(dve):
            for s in seeded:
                dve.sem_inc(s.sem, s.seed)
            dve.memset(stack[:, :, :, :, :, :], 0.0)
            dve.memset(kT[0][64:128, :, :], 0.0)
            dve.memset(kT[1][0:64, :, :], 0.0)
            dve.memset(whot[:, :, :, :, :], 0.0)
            dve.memset(vp[:, :, :, HD:HD + 1], 1.0)
            dve.wait_ge(w_loaded, 160)
            for tab, k in ((cosw, 0), (sinw, 1)):
                for s in range(2):
                    for half in range(2):
                        dve.scalar_tensor_tensor(
                            tab[:, :, s, 4 * half:4 * half + 4], rope[:, :, k, :], float(HD) ** 0.5,
                            qkw[:, s, 4 * half:4 * half + 4].unsqueeze(1).to_broadcast([P, NT, 4]),
                            ALU.mult, ALU.mult)
            dve.wait_ge(set_tr, 4)
            dve.tensor_copy(wqkvT[:, :], S[0][:, 0:3 * P])
            dve.tensor_copy(wprojT[:, :], S[0][:, 3 * P:4 * P]).then_inc(set_ev, 1)
            dve.tensor_copy(downT[:, 0:512], S[1][:, :]).then_inc(set_ev, 1)
            dve.tensor_copy(downT[:, 512:1024], OV[:, :]).then_inc(set_ev, 1)
            dve.tensor_copy(keysT, A[:, :]).then_inc(set_ev, 1)
            dve.wait_ge(set_mm, 1)
            dve.tensor_copy(simW[:, :, :, :].rearrange("p s h k -> p (s h k)"), G[0][:, :]).then_inc(set_w, 1)

            def normalise(b, t):
                dve.wait_ge(sq_done.sem, sq_done.value(b, t + 1))
                dve.tensor_reduce(qk_ms[:, :], qk_s[:, :, :], AX.X, ALU.add).then_inc(ms_done.sem, 1)
                dve.wait_ge(qrs_done.sem, qrs_done.value(b, 2 * t + 2))
                dve.wait_ge(v_done.sem, v_done.value(b, t + 1))
                dve.wait_ge(rope_done.sem, rope_done.value(b, 2 * t))
                dve.tensor_tensor(qk_n[:, :, :], A[:, 0:2 * D].rearrange("p (g d) -> p g d", d=HD),
                                  qk_rs[:, :].unsqueeze(2).to_broadcast([P, 32, HD]), ALU.mult)\
                    .then_inc(qn_done.sem, 1)

            def normalise_o(b, g):
                dve.wait_ge(a_ready.sem, a_filled(b, f"o{g}"))
                heads = A[:, :].rearrange("p (t h c) -> p t h c", t=NT, h=4)
                dve.reciprocal(rden[:, :, :], heads[:, :, :, HD]).then_inc(rden_done.sem, 1)
                dve.wait_ge(rden_done.sem, rden_done.value(b, g + 1))
                dve.tensor_tensor(o[:, :, 4 * g:4 * g + 4, :], heads[:, :, :, 0:HD],
                                  rden[:, :, :].unsqueeze(3).to_broadcast([P, NT, 4, HD]), ALU.mult)\
                    .then_inc(o_done.sem, 1)

            def moments(src, signal, b, n):
                dve.wait_ge(signal.sem, signal.value(b, n))
                for t in range(NT):
                    last = dve.bn_stats(stats[:, t, :], src[:, t, :])
                last.then_inc(signal.sem, 1)
                dve.wait_ge(signal.sem, signal.value(b, n + 1))
                pass_wait(dve)
                for t in range(NT):
                    last = dve.bn_aggr(mv[:, t, :], stats[:, t, :])
                last.then_inc(signal.sem, 1)

            def norm1(b):
                dve.wait_ge(a_ready.sem, a_filled(b, "proj"))
                dve.wait_ge(xr_loaded.sem, xr_loaded.value(b, 16))
                dve.tensor_tensor(r1[:, :, :].rearrange("p t d -> p (t d)"), A[:, :],
                                  xr[:, :, :].rearrange("p t d -> p (t d)"), ALU.add)\
                    .then_inc(ln1.sem, 1)
                moments(r1, ln1, b, 1)
                dve.wait_ge(ln1.sem, ln1.value(b, 10))
                for t in range(NT):
                    last = dve.tensor_scalar(yi[:, t, :], r1[:, t, :], mv[:, t, 0:1], rs[:, 4, t:t + 1],
                                             ALU.subtract, ALU.mult)
                last.then_inc(yi_done.sem, 1)
                for t in range(NT):
                    last = dve.tensor_scalar(y[:, t, :], r1[:, t, :], mv[:, t, 0:1], rs[:, 0, t:t + 1],
                                             ALU.subtract, ALU.mult)
                last.then_inc(ln1.sem, 1)

            def norm2(b):
                bank = bank_f("ffn")
                dve.wait_ge(f_ready.sem, f_filled(b, "ffn"))
                dve.wait_ge(ln1.sem, ln1.value(b, 11))
                dve.wait_ge(out_stored.sem, out_stored.value(b, 0))
                dve.tensor_tensor(r2[:, :, :].rearrange("p t d -> p (t d)"), bank[:, :],
                                  y[:, :, :].rearrange("p t d -> p (t d)"), ALU.add)\
                    .then_inc(ln2.sem, 1)
                moments(r2, ln2, b, 1)
                dve.wait_ge(ln2.sem, ln2.value(b, 5))
                for t in range(NT):
                    last = dve.tensor_scalar(r2[:, t, :], r2[:, t, :], mv[:, t, 0:1], rs[:, 0, t:t + 1],
                                             ALU.subtract, ALU.mult)
                last.then_inc(out_ready.sem, 1)

            def top_keys(b, t):
                dve.wait_ge(sims_done.sem, sims_done.value(b, t + 1))
                pass_wait(dve)
                for s in range(2):
                    for h in range(H):
                        last = dve.max(out=topv[:, t, s, h, :], in_=sims[:, t % 2, s, h, :])
                last.then_inc(topv_done.sem, 1)
                dve.wait_ge(topv_done.sem, topv_done.value(b, t + 1))
                pass_wait(dve)
                for s in range(2):
                    for h in range(H):
                        last = dve.max_index(topi[:, t, s, h, :], topv[:, t, s, h, :], sims[:, t % 2, s, h, :])
                last.then_inc(top1_done.sem, 1)

            def top_pairs(b, t):
                dve.wait_ge(cand_done.sem, cand_done.value(b, t + 1))
                pass_wait(dve)
                for h in range(H):
                    last = dve.max(out=fsel[:, t, h, :], in_=candv[:, t % 2, h, :])
                last.then_inc(fsel_done.sem, 1)
                dve.wait_ge(fsel_done.sem, fsel_done.value(b, t + 1))
                pass_wait(dve)
                for h in range(H):
                    last = dve.max_index(psel[:, t % 2, h, :], fsel[:, t, h, :], candv[:, t % 2, h, :])
                last.then_inc(top2_done.sem, 1)
                dve.wait_ge(top2_done.sem, top2_done.value(b, t + 1))
                dims = [P, H, NCAND, TOPK]
                dve.tensor_tensor(gat[:, t % 2], psel[:, t % 2].unsqueeze(2).to_broadcast(dims),
                                  cand_no[:, :, :].unsqueeze(1).to_broadcast(dims), ALU.is_equal)\
                    .then_inc(hotc_done.sem, 1)

            def selected(b, t):
                dve.wait_ge(gat_done.sem, gat_done.value(b, 2 * t + 2))
                dve.tensor_reduce(esel[:, t, :].rearrange("p (h k) -> p h k", h=H),
                                  gat[:, t % 2, :, 0:10, :].rearrange("p h c k -> p h k c"), AX.X, ALU.add).then_inc(esel_done.sem, 1)

            def decode(b, pair):
                bank = bank_f(f"sel{pair}")
                e, w = bank[:, 0:P], bank[:, P:2 * P]
                dve.wait_ge(f_ready.sem, f_filled(b, f"sel{pair}"))
                dve.tensor_copy(eint[:, pair, :], e)
                dve.tensor_scalar(wpart[:, 0, pair, :], w, 0.0, None, ALU.max).then_inc(dec.sem, 1)
                dve.wait_ge(dec.sem, dec.value(b, 4 * pair + 1))
                dve.tensor_scalar(elo[:, pair, :], eint[:, pair, :], P - 1, None, ALU.bitwise_and)
                dve.tensor_scalar(ehi[:, pair, :], eint[:, pair, :], NEXP - P, None, ALU.bitwise_and)
                dve.scalar_tensor_tensor(wrest[:, pair, :], w, 0.0, wpart[:, 0, pair, :], ALU.max, ALU.subtract)\
                    .then_inc(dec.sem, 1)
                dve.wait_ge(dec.sem, dec.value(b, 4 * pair + 2))
                dve.tensor_copy(wpart[:, 1, pair, :], wrest[:, pair, :]).then_inc(dec.sem, 1)
                dve.wait_ge(dec.sem, dec.value(b, 4 * pair + 3))
                dve.tensor_tensor(wpart[:, 2, pair, :], wrest[:, pair, :], wpart[:, 1, pair, :], ALU.subtract)\
                    .then_inc(dec.sem, 1)

            def one_hots(b, los):
                dve.wait_ge(dec.sem, dec.value(b, 8))
                for lo in los:
                    last = dve.tensor_scalar(onehot[:, lo, :, :], elo[:, :, :], float(lo), None, ALU.is_equal)
                return last

            def hi_one_hots(b):
                for hi in range(NHI):
                    last = dve.tensor_scalar(hot_hi[:, hi, :], ehi[:, :, :].rearrange("p a t -> p (a t)"),
                                             float(hi * P), None, ALU.is_equal)
                last.then_inc(hot_done.sem, 1)

            def weighted_one_hots(b, pair):
                dve.wait_ge(hot_done.sem, hot_done.value(b, 1))
                if pair == 1:
                    dve.wait_ge(g_ready.sem, g_ready.value(b, 4))
                for part in range(3):
                    for i in range(2):
                        rows = slice(64 * i, 64 * i + 64)
                        w = wpart[rows, part, pair, :].unsqueeze(1).to_broadcast([64, NHI, P])
                        last = dve.tensor_tensor(whot[rows, part, i], hot_hi[rows, :, pair * P:pair * P + P], w,
                                                 ALU.mult)
                last.then_inc(hot_done.sem, 1)

            def apply_weights(b, chunk):
                if chunk == 0:
                    dve.wait_ge(hid_done.sem, hid_done.value(b, NHI))
                dve.wait_ge(g_ready.sem, g_ready.value(b, chunk + 1))
                pair, t0 = chunk // 4, chunk % 4 * 32
                h = hid[:, :, :].rearrange("p c (a s t) -> p a s c t", a=2, s=2)[:, pair, :, :, t0:t0 + 32]
                g = G[chunk % 2][:, :].rearrange("p (t s c) -> p s c t", s=2, c=NHI)
                dve.tensor_tensor(h, g, h, ALU.mult).then_inc(g_free.sem, 1)

            def batch(b, f):
                if f is not None:
                    top_keys(f, 0)
                    top_keys(f, 1)
                for t in range(NT):
                    if b is not None:
                        normalise(b, t)
                    if f is not None:
                        if t + 2 < NT:
                            top_keys(f, t + 2)
                        top_pairs(f, t)
                        if t >= 1:
                            selected(f, t - 1)
                if f is not None:
                    selected(f, NT - 1)
                if b is not None:
                    normalise_o(b, 0)
                if f is not None:
                    decode(f, 0)
                    decode(f, 1)
                    one_hots(f, range(P))
                    hi_one_hots(f)
                    weighted_one_hots(f, 0)
                for g in range(1, NG):
                    if b is not None:
                        normalise_o(b, g)
                    if f is not None:
                        if g < NG - 1:
                            apply_weights(f, 2 * g - 2)
                            apply_weights(f, 2 * g - 1)
                        else:
                            weighted_one_hots(f, 1)
                            for chunk in range(4, 8):
                                apply_weights(f, chunk)
                if f is not None:
                    norm2(f)
                if b is not None:
                    norm1(b)

            batch(0, None)
            with dve.Fori(1, BATCH) as b:
                batch(b, b - 1)
            batch(None, BATCH - 1)


_INS = ["L0_attn_x", "L0_attn_w_qkv", "L0_attn_w_proj", "L0_attn_q_norm_w", "L0_attn_k_norm_w", "L0_ffn_w_q",
        "L0_ffn_keys", "L0_ffn_expert_down", "L0_ffn_expert_up", "L0_ffn_norm_w"]


def rope_constants(seq_len, head_dim, theta):
    import numpy as np
    freqs = theta ** (-np.arange(0, head_dim, 2, dtype=np.float32) / head_dim)
    ang = np.arange(seq_len, dtype=np.float32)[:, None] * freqs.astype(np.float32)[None, :]
    return np.stack([np.cos(ang), np.sin(ang)], axis=1).astype(np.float32)


def kernel(**inputs):
    import numpy as np
    import concourse.bacc as bacc
    from concourse import mybir
    from concourse.bass_utils import run_bass_kernel_spmd

    nc = bacc.Bacc("TRN2", target_bir_lowering=False, num_devices=1)
    arrays = {f"in_{n}": np.ascontiguousarray(inputs[n]) for n in _INS}
    arrays["in_rope"] = rope_constants(inputs["L0_attn_x"].shape[1], inputs["L0_attn_q_norm_w"].shape[0], 32.0)
    args = [nc.dram_tensor(n, a.shape, mybir.dt.from_np(a.dtype), kind="ExternalInput").ap()
            for n, a in arrays.items()]
    out = nc.dram_tensor("out", inputs["L0_attn_x"].shape, mybir.dt.float32, kind="ExternalOutput").ap()
    attention_then_peer_layer(nc, *args, out)
    return run_bass_kernel_spmd(nc, [arrays], core_ids=[0]).results[0]["out"]
```

```python
import concourse.bass as bass
from concourse import mybir
from contextlib import ExitStack


class Signal:

    def __init__(self, sem, per_batch, seed=0):
        self.sem, self.per_batch, self.seed = sem, per_batch, seed

    def value(self, b, n):
        assert self.seed + n >= 1 or (isinstance(b, int) and b * self.per_batch + self.seed + n >= 1)
        return b * self.per_batch + (self.seed + n)


def attention_then_peer_layer(nc, x, w_qkv, w_proj, q_norm_w, k_norm_w, w_q, keys, expert_down, expert_up,
                              norm_w, rope_table, out):
    fp32, bf16, fp16, u16, i32 = (
        mybir.dt.float32, mybir.dt.bfloat16, mybir.dt.float16, mybir.dt.uint16, mybir.dt.int32)
    ALU, ACT, AX = mybir.AluOpType, mybir.ActivationFunctionType, mybir.AxisListType

    P = 128
    BATCH, T, D = x.shape
    NT = T // P
    NH, HD = 16, 8
    NPAIR = NH // 2
    SLOTS = 8
    SCALE = float(HD) ** -0.5
    H, NK, TOPK = keys.shape[0], keys.shape[1], 8
    NEXP = expert_down.shape[0]
    NHI = NEXP // P
    NCAND = 20
    SAFE_SCORE = 64.0
    LN_EPS, RMS_EPS = 1e-5, 1e-6
    NEG = -1e30

    KC_AT = [0, 512, 1024, 896]
    PCOLS = 1280
    UNITS = 5 * 2
    NG = NH // 4

    ctx = ExitStack()
    with ctx:
        def sb(name, shape, dt):
            return ctx.enter_context(nc.sbuf_tensor(name, shape, dt))

        def pb(name):
            return ctx.enter_context(nc.psum_tensor(name, [P, 512], fp32))

        def sem(name):
            return ctx.enter_context(nc.semaphore(name))

        ident = sb("ident", [P, P], fp32)
        ident_b = sb("ident_b", [P, P], bf16)
        causal = sb("causal", [P, P], bf16)
        cand_no = sb("cand_no", [P, NCAND, TOPK], u16)
        wqkvT = sb("wqkvT", [P, 3 * D], fp32)
        wprojT = sb("wprojT", [P, D], fp32)
        simW = sb("simW", [P, 2, H, NK], fp32)
        downT = sb("downT", [P, NEXP], fp32)
        up = sb("up", [P, NHI, D], fp32)
        normw = sb("normw", [P, 1], fp32)
        far = sb("far", [P, 1], i32)
        cosw = sb("cosw", [P, NT, 2, HD], fp32)
        sinw = sb("sinw", [P, NT, 2, HD], fp32)
        xa = sb("xa", [P, NT, D], fp32)
        xr = sb("xr", [P, NT, D], fp32)
        xT = sb("xT", [P, T], fp32)
        qk_a = sb("qk_a", [P, 2, 2, NH, HD], fp32)
        qk_n = sb("qk_n", [P, 2, 2, NH, HD], fp32)
        qk_u = sb("qk_u", [P, 2, 2, NH, HD], fp32)
        qk_r = sb("qk_r", [P, 2, 2, NH, HD], fp32)
        qk_ms = sb("qk_ms", [P, 64], fp32)
        qk_rs = sb("qk_rs", [P, 64], fp32)
        qk_t = sb("qk_t", [P, 64], fp32)
        stack = sb("stack", [P, 2, 2, NH, SLOTS, HD], bf16)
        qT = sb("qT", [P, NPAIR, T], bf16)
        kT = [sb("kT_even", [P, NPAIR, T], bf16), sb("kT_odd", [P, NPAIR, T], bf16)]
        vp = sb("vp", [P, NT, NH, HD + 1], fp32)
        prob = sb("prob", [P, 4, PCOLS], fp32)
        xn = sb("xn", [P, T], fp32)
        oT = xn
        rden = sb("rden", [P, NT, 4], fp32)
        r2 = sb("r2", [P, NT, D], fp32)
        o = r2[:, :, :].rearrange("p t (h d) -> p t h d", h=NH)
        oTn = xT
        r1 = xr
        stats = sb("stats", [P, NT, 6], fp32)
        mv = [sb("mv1", [P, NT, 2], fp32), sb("mv2", [P, NT, 2], fp32)]
        var = [sb("var1", [P, 2, NT], fp32), sb("var2", [P, 1, NT], fp32)]
        rs = [sb("rs1", [P, 2, NT], fp32), sb("rs2", [P, 1, NT], fp32)]
        rs_t = sb("rs_t", [P, 2, NT], fp32)
        y = sb("y", [P, NT, D], fp32)
        yi = sb("yi", [P, NT, D], fp32)
        sims = sb("sims", [P, 2, 2, H, NK], fp32)
        topv = sb("topv", [P, NT, 2, H, TOPK], fp32)
        topi = sb("topi", [P, NT, 2, H, TOPK], u16)
        i12 = sb("i12", [P, 2, H, TOPK], fp16)
        candv = sb("candv", [P, 2, H, NCAND], fp32)
        cande = sb("cande", [P, 2, H, NCAND], fp16)
        fsel = sb("fsel", [P, NT, H, TOPK], fp32)
        psel = sb("psel", [P, 2, H, TOPK], u16)
        gat = sb("gat", [P, 2, H, NCAND, TOPK], fp16)
        esel = sb("esel", [P, NT, H * TOPK], fp32)
        eint = sb("eint", [P, 2, P], u16)
        elo = sb("elo", [P, 2, P], u16)
        ehi = sb("ehi", [P, 2, P], u16)
        wpart = sb("wpart", [P, 3, 2, P], bf16)
        wrest = sb("wrest", [P, 2, P], fp32)
        onehot = sb("onehot", [P, P, 2, P], bf16)
        hot_hi = sb("hot_hi", [P, NHI, 2 * P], bf16)
        whot = sb("whot", [P, 3, 2, NHI, P], bf16)
        hid = sb("hid", [P, NHI, T], fp32)

        tmp = onehot[:, :, :, :].rearrange("p a b c -> p (a b c)").bitcast(fp32)
        wq_raw = tmp[:, 0:2048].rearrange("p (g d) -> p g d", g=16)
        keys_raw = tmp[:, 2048:2560].rearrange("p (c s d) -> p c s d", c=2, s=2)
        keysT = tmp[:, 2560:3072]
        wqkv_raw = tmp[:, 3072:3456].rearrange("p (g d) -> p g d", g=3)
        wproj_raw = tmp[:, 3456:3584]
        down_raw = tmp[:, 3584:4608].rearrange("p (g d) -> p g d", g=8)
        rope = tmp[:, 4608:4640].rearrange("p (t c d) -> p t c d", t=NT, c=2)
        qkw = tmp[:, 4640:4656].rearrange("p (s d) -> p s d", s=2)

        qkw_sq = tmp[:, 4656:4672].rearrange("p (s d) -> p s d", s=2)
        pair_sq = tmp[:, 4672:4680].rearrange("p (s d) -> p s d", s=2)
        score_sq = tmp[:, 4680:4684]
        most_sq = tmp[:, 4684:4685]
        peak, peak_rest = (x[:, :].rearrange("p (t h) -> p t h", t=NT) for x in (qk_t, qk_ms))
        shift = qk_u[:, :, :, :, :].rearrange("p s t h d -> p (s t h d)").bitcast(bf16)\
            .rearrange("p (h c d) -> p h c d", h=NH, c=SLOTS)

        S = [pb("S0"), pb("S1")]
        OV = pb("OV")
        A = pb("A")
        F = [pb("F0"), pb("F1")]
        G = [pb("G0"), pb("G1")]
        A_b = A[:, :].bitcast(bf16).rearrange("p (j t) -> p j t", j=NPAIR)

        w_loaded, const_done, zero_done = sem("w_loaded"), sem("const_done"), sem("zero_done")
        set_tr, set_ev, set_mm, set_w = sem("set_tr"), sem("set_ev"), sem("set_mm"), sem("set_w")

        waits_passed = sem("waits_passed")

        ROOT_STEPS = 11

        def signal(name, per_batch, seed=0):
            return Signal(sem(name), per_batch, seed)

        xa_loaded = signal("xa_loaded", 16)
        xr_loaded = signal("xr_loaded", 16)
        out_stored = signal("out_stored", 16, 32)
        a_ready = signal("a_ready", 19)
        xT_done = signal("xT_done", 1)
        sq_done = signal("sq_done", NT)
        v_done = signal("v_done", NT)
        ms_done = signal("ms_done", 2)
        qroot = signal("qroot", 2 * (1 + ROOT_STEPS))
        qn_done = signal("qn_done", 2)
        rope_done = signal("rope_done", 8)
        rot_done = signal("rot_done", 4, 1)
        first_done = signal("first_done", 2)
        rest_done = signal("rest_done", 2)
        second_done = signal("second_done", 2)
        stack_done = signal("stack_done", 2, 1)
        qT_done = signal("qT_done", NT)
        kT_done = signal("kT_done", NT)
        s_ready = signal("s_ready", NG * UNITS)
        exp_done = signal("exp_done", NG * UNITS, 2)
        pv_done = signal("pv_done", NG, 1)
        oT_done = signal("oT_done", NG, 1)
        rden_done = signal("rden_done", NG)
        o_done = signal("o_done", NG)
        oTn_done = signal("oTn_done", 1)
        ln1 = signal("ln1", 5 + ROOT_STEPS, 5 + ROOT_STEPS)
        yi_done = signal("yi_done", 1)
        f_ready = signal("f_ready", 14)
        xn_done = signal("xn_done", 1)
        sims_done = signal("sims_done", NT)
        topv_done = signal("topv_done", NT)
        top1_done = signal("top1_done", NT, 2)
        i12_done = signal("i12_done", NT)
        cand_done = signal("cand_done", NT, 1)
        fsel_done = signal("fsel_done", NT)
        top2_done = signal("top2_done", NT)
        hotc_done = signal("hotc_done", NT)
        gat_done = signal("gat_done", 2 * NT)
        esel_done = signal("esel_done", NT)
        hid_done = signal("hid_done", NHI, 1)
        dec = signal("dec", 4, 4)
        hot_done = signal("hot_done", 3)
        g_ready = signal("g_ready", 8)
        g_free = signal("g_free", 8, 2)
        r2_done = signal("r2_done", 1)
        ffn_ready = signal("ffn_ready", 1)
        ln2 = signal("ln2", 4 + ROOT_STEPS, 2 * (4 + ROOT_STEPS))
        out_ready = signal("out_ready", 1)
        seeded = [out_stored, hid_done, rot_done, stack_done, exp_done, pv_done, oT_done, ln1, dec, ln2, cand_done, top1_done, g_free]

        peak_ready = signal("peak_ready", NT * NH)
        peak_done = signal("peak_done", NT * NH)
        shift_steps = signal("shift_steps", 1 + 4 * NT)
        shift_turned = signal("shift_turned", NT)
        shift_added = signal("shift_added", NT)
        bound_steps = sem("bound_steps")

        A_USES = [("xT", [(xT_done, 1)])]
        for half in range(2):
            A_USES += [(f"qkv{t}", [(v_done, t + 1)]) for t in (2 * half, 2 * half + 1)]
        for t in range(NT):
            A_USES += [(f"Q{t}", [(qT_done, t + 1)]), (f"K{t}", [(kT_done, t + 1)])]
        A_USES += [(f"o{g}", [(o_done, g + 1)]) for g in range(NG)]
        A_USES += [("oTn", [(oTn_done, 1)]), ("proj", [(ln1, 1)])]
        F_USES = [("xn", [(xn_done, 1)])]
        F_USES += [(f"sims{t}", [(sims_done, t + 1)]) for t in range(NT)]
        F_USES += [(f"hid{c}", [(hid_done, c + 1)]) for c in range(NHI)]
        F_USES += [("sel", [(dec, 2)])]

        def pass_wait(eng):
            eng.sem_inc(waits_passed, 1)

        def number(uses, use):
            return [name for name, _ in uses].index(use)

        def wait_read(eng, b, uses, i):
            for s, n in uses[i][1]:
                eng.wait_ge(s.sem, s.value(b, n - s.per_batch if i < 0 else n))

        def a_filled(b, use):
            return a_ready.value(b, number(A_USES, use) + 1)

        def wait_a_empty(eng, b, use):
            wait_read(eng, b, A_USES, number(A_USES, use) - 1)

        def bank_f(use):
            return F[number(F_USES, use) % 2]

        def f_filled(b, use):
            return f_ready.value(b, number(F_USES, use) + 1)

        def wait_f_empty(eng, b, use):
            wait_read(eng, b, F_USES, number(F_USES, use) - 2)

        SCORES = [[(0, 0, 0)], [(0, 1, 0), (0, 3, 384)], [(0, 2, 0), (1, 2, 256)],
                  [(1, 0, 0)], [(1, 1, 0), (1, 3, 384)]]

        block = ctx.enter_context(nc.Block())

        @block.sync
        def _(sp):
            loads = [
                (wq_raw, w_q.rearrange("(g p) d -> p g d", p=P)),
                (keys_raw, keys.rearrange("(c h) k s d -> (h k) c s d", c=2)),
                (wqkv_raw, w_qkv.rearrange("(g p) d -> p g d", p=P)),
                (wproj_raw, w_proj),
                (down_raw, expert_down.rearrange("(g p) d -> p g d", p=P)),
                (up[:, :, :], expert_up.rearrange("(g p) d -> p g d", p=P)),
                (normw[:, :], norm_w.rearrange("(p a) -> p a", a=1)),
                (qkw[:, 0, :], q_norm_w.rearrange("(a n) -> a n", a=1).to_broadcast([P, HD])),
                (qkw[:, 1, :], k_norm_w.rearrange("(a n) -> a n", a=1).to_broadcast([P, HD])),
                (rope[:, :, :, :], rope_table.rearrange("(t p) c d -> p t c d", p=P)),
            ]
            for dst, src in loads:
                sp.dma_start(dst, src).then_inc(w_loaded, 16)

            def load_xa(b):
                sp.dma_start(xa[:, :, :], x[b].rearrange("(t p) d -> p t d", p=P)).then_inc(xa_loaded.sem, 16)

            def load_xr(b):
                sp.dma_start(xr[:, :, :], x[b].rearrange("(t p) d -> p t d", p=P)).then_inc(xr_loaded.sem, 16)

            def store(b):
                sp.wait_ge(out_ready.sem, out_ready.value(b, 1))
                sp.dma_start(out[b].rearrange("(t p) d -> p t d", p=P), r2[:, :, :]).then_inc(out_stored.sem, 16)

            def next_xa(b):
                sp.wait_ge(a_ready.sem, a_filled(b, "xT"))
                load_xa(b + 1)

            def next_xr(b):
                sp.wait_ge(ln1.sem, ln1.value(b, ln1.per_batch))
                load_xr(b + 1)

            load_xa(0)
            load_xr(0)
            next_xa(0)
            next_xr(0)
            with sp.Fori(1, BATCH - 1) as b:
                next_xa(b)
                store(b - 1)
                next_xr(b)
            store(BATCH - 2)
            store(BATCH - 1)
            sp.wait_ge(out_stored.sem, out_stored.value(BATCH - 1, 16))

        @block.gpsimd
        def _(pool):
            pool.memset(ident[:, :], 0.0).then_inc(zero_done, 1)
            pool.memset(ident_b[:, :], 0.0).then_inc(zero_done, 1)
            pool.memset(causal[:, :], 0.0).then_inc(zero_done, 1)
            pool.wait_ge(zero_done, 3)
            for m in (ident, ident_b):
                pool.affine_select(out=m[:, :], in_=m[:, :], compare_op=ALU.not_equal, fill=1.0, base=0,
                                   pattern=[[-1, P]], channel_multiplier=1).then_inc(const_done, 1)
            pool.affine_select(out=causal[:, :], in_=causal[:, :], compare_op=ALU.is_ge, fill=NEG, base=0,
                               pattern=[[1, P]], channel_multiplier=-1).then_inc(const_done, 1)
            pool.iota(cand_no[:, :, :], pattern=[[1, NCAND], [0, TOPK]], base=0, channel_multiplier=0).then_inc(const_done, 1)
            pool.wait_ge(const_done, 4)

            def rotate(b, half):
                pool.wait_ge(qn_done.sem, qn_done.value(b, half + 1))
                pool.wait_ge(stack_done.sem, stack_done.value(b, half))
                for i in range(2):
                    for dst, tab in ((qk_a, cosw), (qk_u, sinw)):
                        w = tab[:, 2 * half + i].unsqueeze(2).to_broadcast([P, 2, NH, HD])
                        pool.tensor_tensor(dst[:, :, i], qk_n[:, :, i], w, ALU.mult).then_inc(rope_done.sem, 1)
                pool.wait_ge(rope_done.sem, rope_done.value(b, 4 * half + 4))
                a, u, r = (x[:, :, :, :, :].rearrange("p s t h d -> p (s t h) d") for x in (qk_a, qk_u, qk_r))
                pool.tensor_tensor(r[:, :, 0:4], a[:, :, 0:4], u[:, :, 4:8], ALU.subtract).then_inc(rot_done.sem, 1)
                pool.tensor_tensor(r[:, :, 4:8], a[:, :, 4:8], u[:, :, 0:4], ALU.add).then_inc(rot_done.sem, 1)

            def split(b, half):
                st = stack[:, :, :, :, :, :].rearrange("p s t h c d -> p (s t h) c d")
                u, r = (x[:, :, :, :, :].rearrange("p s t h d -> p (s t h) d") for x in (qk_u, qk_r))
                pool.wait_ge(first_done.sem, first_done.value(b, half + 1))
                pool.tensor_tensor(u, r, st[:, :, 2, :], ALU.subtract).then_inc(rest_done.sem, 1)
                pool.wait_ge(second_done.sem, second_done.value(b, half + 1))
                pool.tensor_tensor(st[:, 0:32, 4, :], u[:, 0:32], st[:, 0:32, 5, :], ALU.subtract)
                pool.tensor_tensor(st[:, 32:64, 0, :], u[:, 32:64], st[:, 32:64, 5, :], ALU.subtract)\
                    .then_inc(stack_done.sem, 1)

            def candidates(b, t):
                pool.wait_ge(top1_done.sem, top1_done.value(b, t + 1))
                pool.wait_ge(cand_done.sem, cand_done.value(b, t))
                pass_wait(pool)
                for side, scale in enumerate((NK, 1)):
                    last = pool.tensor_scalar(i12[:, side], topi[:, t, side], float(scale), None, ALU.mult)
                last.then_inc(i12_done.sem, 1)
                pool.wait_ge(i12_done.sem, i12_done.value(b, t + 1))
                last = None
                for dst, one, two in ((candv, topv[:, t, 0], topv[:, t, 1]), (cande, i12[:, 0], i12[:, 1])):
                    c = dst[:, t % 2]
                    pool.tensor_tensor(c[:, :, 0:8], one[:, :, 0:1].to_broadcast([P, H, 8]), two, ALU.add)
                    pool.tensor_tensor(c[:, :, 8:12], one[:, :, 1:2].to_broadcast([P, H, 4]), two[:, :, 0:4],
                                       ALU.add)
                    pool.tensor_tensor(c[:, :, 12:16].rearrange("p h (a b) -> p h a b", a=2),
                                       one[:, :, 2:4].unsqueeze(3).to_broadcast([P, H, 2, 2]),
                                       two[:, :, 0:2].unsqueeze(2).to_broadcast([P, H, 2, 2]), ALU.add)
                    last = pool.tensor_tensor(c[:, :, 16:20], one[:, :, 4:8],
                                              two[:, :, 0:1].to_broadcast([P, H, 4]), ALU.add)
                last.then_inc(cand_done.sem, 1)

            def gather(b, t):
                pool.wait_ge(hotc_done.sem, hotc_done.value(b, t + 1))
                g = gat[:, t % 2]
                pool.tensor_tensor(g, g, cande[:, t % 2].unsqueeze(3).to_broadcast([P, H, NCAND, TOPK]), ALU.mult)\
                    .then_inc(gat_done.sem, 1)
                pool.wait_ge(gat_done.sem, gat_done.value(b, 2 * t + 1))
                pool.tensor_tensor(g[:, :, 0:10], g[:, :, 0:10], g[:, :, 10:20], ALU.add)\
                    .then_inc(gat_done.sem, 1)

            def iteration(b, nxt):
                if b is not None:
                    candidates(b, 0)
                if nxt is not None:
                    rotate(nxt, 0)
                    split(nxt, 0)
                if b is not None:
                    candidates(b, 1)
                    gather(b, 0)
                    candidates(b, 2)
                if nxt is not None:
                    rotate(nxt, 1)
                    split(nxt, 1)
                if b is not None:
                    gather(b, 1)
                    candidates(b, 3)
                    gather(b, 2)
                    gather(b, 3)

            iteration(None, 0)
            with pool.Fori(0, BATCH - 1) as b:
                iteration(b, b + 1)
            iteration(BATCH - 1, None)

        @block.scalar
        def _(act):
            act.wait_ge(w_loaded, 160)

            def normed(b):
                act.wait_ge(f_ready.sem, f_filled(b, "xn"))
                bank = bank_f("xn")
                act.activation(xn[:, :], bank[:, :], ACT.Copy, scale=normw[:, 0:1]).then_inc(xn_done.sem, 1)

            def similarities(b, t):
                act.wait_ge(f_ready.sem, f_filled(b, f"sims{t}"))
                act.wait_ge(top1_done.sem, top1_done.value(b, t - 1))
                bank = bank_f(f"sims{t}")
                act.activation(sims[:, t % 2].rearrange("p s h k -> p (s h k)"), bank[:, :], ACT.Copy)\
                    .then_inc(sims_done.sem, 1)

            def hidden(b, c):
                act.wait_ge(f_ready.sem, f_filled(b, f"hid{c}"))
                bank = bank_f(f"hid{c}")
                act.activation(hid[:, c, :], bank[:, :], ACT.Gelu).then_inc(hid_done.sem, 1)

            def taken_qkv(b, t):
                act.wait_ge(a_ready.sem, a_filled(b, f"qkv{t}"))
                act.wait_ge(rot_done.sem, rot_done.value(b, t // 2 * 2))
                sides = A[:, 0:2 * D].rearrange("p (s h d) -> p s h d", s=2, h=NH)
                act.activation(qk_a[:, :, t % 2], sides, ACT.Square)
                act.activation(qk_n[:, :, t % 2], sides, ACT.Copy).then_inc(sq_done.sem, 1)
                act.activation(vp[:, t, :, 0:HD], A[:, 2 * D:3 * D].rearrange("p (h d) -> p h d", h=NH), ACT.Copy)\
                    .then_inc(v_done.sem, 1)

            def first_parts(b, half):
                st = stack[:, :, :, :, :, :].rearrange("p s t h c d -> p (s t h) c d")
                r = qk_r[:, :, :, :, :].rearrange("p s t h d -> p (s t h) d").unsqueeze(2)\
                    .to_broadcast([P, 64, 3, HD])
                act.wait_ge(rot_done.sem, rot_done.value(b, 2 * half + 2))
                act.activation(st[:, 0:32, 0:3, :], r[:, 0:32], ACT.Copy)
                act.activation(st[:, 32:64, 2:5, :], r[:, 32:64], ACT.Copy).then_inc(first_done.sem, 1)

            def second_parts(b, half):
                st = stack[:, :, :, :, :, :].rearrange("p s t h c d -> p (s t h) c d")
                u = qk_u[:, :, :, :, :].rearrange("p s t h d -> p (s t h) d").unsqueeze(2)\
                    .to_broadcast([P, 64, 2, HD])
                act.wait_ge(rest_done.sem, rest_done.value(b, half + 1))
                act.activation(st[:, 0:32, 3:6:2, :], u[:, 0:32], ACT.Copy)
                act.activation(st[:, 32:64, 1:6:4, :], u[:, 32:64], ACT.Copy).then_inc(second_done.sem, 1)

            def transposed(b, t):
                act.wait_ge(a_ready.sem, a_filled(b, f"Q{t}"))
                act.activation(qT[:, :, t * P:(t + 1) * P], A_b, ACT.Copy).then_inc(qT_done.sem, 1)
                act.wait_ge(a_ready.sem, a_filled(b, f"K{t}"))
                act.activation(kT[0][0:64, :, t * P:(t + 1) * P], A_b[0:64], ACT.Copy)
                act.activation(kT[1][64:128, :, t * P:(t + 1) * P], A_b[64:128], ACT.Copy).then_inc(kT_done.sem, 1)

            def exps(b, g):
                act.wait_ge(pv_done.sem, pv_done.value(b, g))
                for u in range(UNITS):
                    n = g * UNITS + u
                    act.wait_ge(s_ready.sem, s_ready.value(b, n + 1))
                    h = 2 * (u // 5)
                    src = S[n % 2][:, :]
                    if u % 5 == 2:
                        dst = prob[:, h:h + 2, KC_AT[2]:KC_AT[2] + 256]
                        src = src.rearrange("p (h n) -> p h n", h=2)
                    else:
                        h, at = (h + u % 5 // 3, 0 if u % 5 in (0, 3) else 512)
                        dst = prob[:, h, at:at + 512]
                    act.activation(dst, src, ACT.Exp, scale=SCALE).then_inc(exp_done.sem, 1)

            def attended(b, g):
                act.wait_ge(pv_done.sem, pv_done.value(b, g + 1))
                if g:
                    act.wait_ge(a_ready.sem, a_filled(b, f"o{g - 1}"))
                act.activation(oT[:, :], OV[:, :], ACT.Copy).then_inc(oT_done.sem, 1)

            def iteration(b, nxt):
                if b is not None:
                    for g in range(NG):
                        exps(b, g)
                        attended(b, g)
                    act.wait_ge(a_ready.sem, a_filled(b, "oTn"))
                    act.activation(oTn[:, :], A[:, :], ACT.Copy).then_inc(oTn_done.sem, 1)
                    normed(b)
                    similarities(b, 0)
                    similarities(b, 1)
                if nxt is not None:
                    act.wait_ge(a_ready.sem, a_filled(nxt, "xT"))
                    act.activation(xT[:, :], A[:, :], ACT.Copy).then_inc(xT_done.sem, 1)
                    taken_qkv(nxt, 0)
                    taken_qkv(nxt, 1)
                if b is not None:
                    similarities(b, 2)
                if nxt is not None:
                    first_parts(nxt, 0)
                    taken_qkv(nxt, 2)
                    taken_qkv(nxt, 3)
                    second_parts(nxt, 0)
                if b is not None:
                    similarities(b, 3)
                if nxt is not None:
                    transposed(nxt, 0)
                    transposed(nxt, 1)
                    first_parts(nxt, 1)
                    second_parts(nxt, 1)
                    transposed(nxt, 2)
                    transposed(nxt, 3)
                if b is not None:
                    for c in range(NHI):
                        hidden(b, c)

            iteration(None, 0)
            with act.Fori(0, BATCH - 1) as b:
                iteration(b, b + 1)
            iteration(BATCH - 1, None)

        @block.tensor
        def _(pe):
            pe.wait_ge(w_loaded, 160)
            pe.wait_ge(const_done, 4)
            raw = ([wqkv_raw[:, g, :] for g in range(3)] + [wproj_raw] + [down_raw[:, g, :] for g in range(8)]
                   + [keys_raw[:, c, s, :] for s in range(2) for c in range(2)])
            for bank, quad in zip((S[0], S[1], OV, A), range(4)):
                for i in range(4):
                    last = nc.tensor.transpose(bank[:, i * P:(i + 1) * P], raw[4 * quad + i], ident[:, :])
                last.then_inc(set_tr, 1)
            pe.wait_ge(set_ev, 4)
            for s in range(2):
                for h in range(H):
                    col = (s * H + h) * NK
                    last = nc.tensor.matmul(G[0][:, col:col + NK], wq_raw[:, 2 * h + s, :],
                                            keysT[:, col:col + NK], start=True, stop=True)
            last.then_inc(set_mm, 1)
            pe.wait_ge(set_w, 1)

            pe.wait_ge(bound_steps, 5)
            far_scores = pe.value_load(far[0:1, 0:1], min_val=0, max_val=1)

            def transpose_x(b):
                pe.wait_ge(xa_loaded.sem, xa_loaded.value(b, 16))
                wait_a_empty(pe, b, "xT")
                for t in range(NT):
                    last = nc.tensor.transpose(A[:, t * P:(t + 1) * P], xa[:, t, :], ident[:, :])
                last.then_inc(a_ready.sem, 1)

            def project_qkv(b, t):
                if t == 0:
                    pe.wait_ge(xT_done.sem, xT_done.value(b, 1))
                wait_a_empty(pe, b, f"qkv{t}")
                nc.tensor.matmul(A[:, 0:3 * D], xT[:, t * P:(t + 1) * P], wqkvT[:, :], start=True, stop=True)\
                    .then_inc(a_ready.sem, 1)

            def transpose_stack(b, t):
                pe.wait_ge(stack_done.sem, stack_done.value(b, t // 2 + 1))
                for side, use in enumerate("QK"):
                    wait_a_empty(pe, b, f"{use}{t}")
                    st = stack[:, side, t % 2].rearrange("p (j h) s d -> p j (h s d)", h=2)
                    for j in range(NPAIR):
                        last = nc.tensor.transpose(A_b[:, j, :], st[:, j, :], ident_b[:, :])
                    last.then_inc(a_ready.sem, 1)

            def shift_by_maxima(b):
                pe.wait_ge(kT_done.sem, kT_done.value(b, NT))
                for t in range(NT):
                    keys_up_to = (t + 1) * P
                    for h in range(NH):
                        n = t * NH + h
                        if n:
                            pe.wait_ge(peak_done.sem, peak_done.value(b, n))
                        nc.tensor.matmul(A[:, 0:keys_up_to], qT[:, h // 2, t * P:keys_up_to],
                                         kT[h % 2][:, h // 2, 0:keys_up_to], start=True, stop=False,
                                         skip_group_check=True)
                        nc.tensor.matmul(A[:, t * P:keys_up_to], causal[:, :], ident_b[:, :], start=False,
                                         stop=True, skip_group_check=True).then_inc(peak_ready.sem, 1)
                pe.wait_ge(peak_done.sem, peak_done.value(b, NT * NH))
                for t in range(NT):
                    pe.wait_ge(shift_steps.sem, shift_steps.value(b, 1 + 4 * (t + 1)))
                    if t:
                        pe.wait_ge(shift_added.sem, shift_added.value(b, t))
                    st = shift.rearrange("p (j h) c d -> p j (h c d)", h=2)
                    for j in range(NPAIR):
                        last = nc.tensor.transpose(A_b[:, j, :], st[:, j, :], ident_b[:, :])
                    last.then_inc(shift_turned.sem, 1)
                pe.wait_ge(shift_added.sem, shift_added.value(b, NT))

            def scores(b, g, units):
                if g == 0:
                    pe.wait_ge(kT_done.sem, kT_done.value(b, NT))
                for u in units:
                    n = g * UNITS + u
                    pe.wait_ge(exp_done.sem, exp_done.value(b, n - 1))
                    j = 2 * g + u // 5
                    bank = S[n % 2]
                    for half, kc, col in SCORES[u % 5]:
                        pe_k = kT[half][:, j, kc * P:(kc + 1) * P]
                        nc.tensor.matmul(bank[:, col:col + T - kc * P], pe_k, qT[:, j, kc * P:T],
                                         start=True, stop=False, skip_group_check=True)
                        last = nc.tensor.matmul(bank[:, col:col + P], ident_b[:, :], causal[:, :],
                                                start=False, stop=True, skip_group_check=True)
                    last.then_inc(s_ready.sem, 1)

            def attend(b, g):
                pe.wait_ge(exp_done.sem, exp_done.value(b, (g + 1) * UNITS))
                pe.wait_ge(oT_done.sem, oT_done.value(b, g))
                if g == 0:
                    pe.wait_ge(ln2.sem, ln2.value(b, 1 - 2 * ln2.per_batch))
                for kc in range(NT):
                    for i in range(4):
                        last = nc.tensor.matmul(
                            OV[32 * i:32 * i + HD + 1, kc * P:T], vp[:, kc, 4 * g + i, :],
                            prob[:, i, KC_AT[kc]:KC_AT[kc] + T - kc * P], start=(kc == 0), stop=(kc == NT - 1),
                            skip_group_check=True)
                last.then_inc(pv_done.sem, 1)

            def transpose_o(b, g):
                pe.wait_ge(oT_done.sem, oT_done.value(b, g + 1))
                wait_a_empty(pe, b, f"o{g}")
                for t in range(NT):
                    last = nc.tensor.transpose(A[:, t * P:(t + 1) * P], oT[:, t * P:(t + 1) * P], ident[:, :])
                last.then_inc(a_ready.sem, 1)

            def project_out(b):
                pe.wait_ge(o_done.sem, o_done.value(b, NG))
                wait_a_empty(pe, b, "oTn")
                for t in range(NT):
                    last = nc.tensor.transpose(A[:, t * P:(t + 1) * P],
                                               o[:, t].rearrange("p h d -> p (h d)"), ident[:, :])
                last.then_inc(a_ready.sem, 1)
                pe.wait_ge(oTn_done.sem, oTn_done.value(b, 1))
                wait_a_empty(pe, b, "proj")
                for t in range(NT):
                    last = nc.tensor.matmul(A[:, t * P:(t + 1) * P], oTn[:, t * P:(t + 1) * P], wprojT[:, :],
                                            start=True, stop=True)
                last.then_inc(a_ready.sem, 1)

            def project_similarities(b, t):
                bank = bank_f(f"sims{t}")
                wait_f_empty(pe, b, f"sims{t}")
                nc.tensor.matmul(bank[:, :], xn[:, t * P:(t + 1) * P],
                                 simW[:, :, :, :].rearrange("p s h k -> p (s h k)"), start=True, stop=True)\
                    .then_inc(f_ready.sem, 1)

            def transpose_yi(b):
                bank = bank_f("xn")
                pe.wait_ge(yi_done.sem, yi_done.value(b, 1))
                wait_f_empty(pe, b, "xn")
                for t in range(NT):
                    last = nc.tensor.transpose(bank[:, t * P:(t + 1) * P], yi[:, t, :], ident[:, :])
                last.then_inc(f_ready.sem, 1)
                pe.wait_ge(xn_done.sem, xn_done.value(b, 1))

            def hidden_products(b):
                for c in range(NHI):
                    bank = bank_f(f"hid{c}")
                    wait_f_empty(pe, b, f"hid{c}")
                    nc.tensor.matmul(bank[:, :], downT[:, c * P:(c + 1) * P], xn[:, :], start=True, stop=True)\
                        .then_inc(f_ready.sem, 1)

            def transpose_selection(b):
                bank = bank_f("sel")
                pe.wait_ge(esel_done.sem, esel_done.value(b, NT))
                wait_f_empty(pe, b, "sel")
                for pair in range(2):
                    two = slice(2 * pair, 2 * pair + 2)
                    nc.tensor.transpose(bank[:, pair * P:(pair + 1) * P],
                                        esel[:, two, :].rearrange("p t k -> p (t k)"), ident[:, :])
                    last = nc.tensor.transpose(bank[:, (2 + pair) * P:(3 + pair) * P],
                                               fsel[:, two].rearrange("p t h k -> p (t h k)"), ident[:, :])
                last.then_inc(f_ready.sem, 1)

            def weights(b, chunk):
                if chunk % 4 == 0:
                    pe.wait_ge(hot_done.sem, hot_done.value(b, 2 + chunk // 4))
                pe.wait_ge(g_free.sem, g_free.value(b, chunk - 1))
                pair, bank = chunk // 4, G[chunk % 2]
                for i in range(32):
                    t = chunk % 4 * 32 + i
                    for part in range(3):
                        last = nc.tensor.matmul(bank[:, 16 * i:16 * i + 16], onehot[:, :, pair, t],
                                                whot[:, part, :, :, t],
                                                start=(part == 0), stop=(part == 2))
                last.then_inc(g_ready.sem, 1)

            def expert_outputs(b):
                pe.wait_ge(g_free.sem, g_free.value(b, 8))
                pe.wait_ge(oT_done.sem, oT_done.value(b, NG if isinstance(b, int) and b == BATCH - 1 else 2 * NG))
                for t in range(NT):
                    for c in range(NHI):
                        last = nc.tensor.matmul(OV[:, t * P:(t + 1) * P], hid[:, c, t * P:(t + 1) * P],
                                                up[:, c, :], start=(c == 0), stop=(c == NHI - 1))
                last.then_inc(ffn_ready.sem, 1)

            def iteration(b, late, nxt):
                if b is not None:
                    scores(b, 0, range(UNITS))
                    for g in range(1, NG):
                        scores(b, g, range(0, 2))
                        attend(b, g - 1)
                        scores(b, g, range(2, UNITS))
                        transpose_o(b, g - 1)
                    attend(b, NG - 1)
                    transpose_o(b, NG - 1)
                    project_out(b)
                if nxt is not None:
                    transpose_x(nxt)
                if b is not None:
                    transpose_yi(b)
                    for t in range(NT):
                        project_similarities(b, t)
                if late is not None:
                    weights(late, 0)
                if nxt is not None:
                    project_qkv(nxt, 0)
                    project_qkv(nxt, 1)
                if late is not None:
                    weights(late, 1)
                    weights(late, 2)
                if nxt is not None:
                    project_qkv(nxt, 2)
                    project_qkv(nxt, 3)
                if late is not None:
                    weights(late, 3)
                if nxt is not None:
                    transpose_stack(nxt, 0)
                    transpose_stack(nxt, 1)
                if late is not None:
                    for chunk in range(4, 8):
                        weights(late, chunk)
                if nxt is not None:
                    transpose_stack(nxt, 2)
                    transpose_stack(nxt, 3)
                    with pe.If(far_scores != 0):
                        shift_by_maxima(nxt)
                if late is not None:
                    expert_outputs(late)
                if b is not None:
                    hidden_products(b)
                    transpose_selection(b)

            iteration(None, None, 0)
            iteration(0, None, 1)
            with pe.Fori(1, BATCH - 1) as b:
                iteration(b, b - 1, b + 1)
            iteration(BATCH - 1, BATCH - 2, None)
            iteration(None, BATCH - 1, None)

        @block.vector
        def _(dve):
            for s in seeded:
                dve.sem_inc(s.sem, s.seed)
            spare = (SLOTS - 2) * HD
            rows = stack[:, :, :, :, :, :].rearrange("p s t h c d -> p s (t h) (c d)")
            dve.memset(rows[:, 0, :, spare:], 0.0)
            dve.memset(rows[:, 1, :, spare + 3:], 0.0)
            dve.memset(rows[:, 1, :, spare:spare + 3], 1.0)
            dve.memset(kT[0][64:128, :, :], 0.0)
            dve.memset(kT[1][0:64, :, :], 0.0)
            dve.memset(whot[:, :, :, :, :], 0.0)
            dve.memset(vp[:, :, :, HD:HD + 1], 1.0)
            dve.wait_ge(w_loaded, 160)
            for tab, k in ((cosw, 0), (sinw, 1)):
                for s in range(2):
                    for half in range(2):
                        dve.scalar_tensor_tensor(
                            tab[:, :, s, 4 * half:4 * half + 4], rope[:, :, k, :], float(HD) ** 0.5,
                            qkw[:, s, 4 * half:4 * half + 4].unsqueeze(1).to_broadcast([P, NT, 4]),
                            ALU.mult, ALU.mult)
            dve.tensor_tensor(qkw_sq, qkw, qkw, ALU.mult).then_inc(bound_steps, 1)
            dve.wait_ge(bound_steps, 1)
            dve.tensor_tensor(pair_sq, qkw_sq[:, :, 0:4], qkw_sq[:, :, 4:8], ALU.max).then_inc(bound_steps, 1)
            dve.wait_ge(bound_steps, 2)
            dve.tensor_tensor(score_sq, pair_sq[:, 0, :], pair_sq[:, 1, :], ALU.mult).then_inc(bound_steps, 1)
            dve.wait_ge(bound_steps, 3)
            dve.tensor_reduce(most_sq, score_sq, AX.X, ALU.max).then_inc(bound_steps, 1)
            dve.wait_ge(bound_steps, 4)
            dve.tensor_scalar(far[:, :], most_sq, (SAFE_SCORE / (SCALE * HD)) ** 2, None, ALU.is_gt)\
                .then_inc(bound_steps, 1)
            dve.wait_ge(bound_steps, 5)
            far_scores = dve.value_load(far[0:1, 0:1], min_val=0, max_val=1)
            dve.wait_ge(set_tr, 4)
            dve.tensor_copy(wqkvT[:, :], S[0][:, 0:3 * P])
            dve.tensor_copy(wprojT[:, :], S[0][:, 3 * P:4 * P]).then_inc(set_ev, 1)
            dve.tensor_copy(downT[:, 0:512], S[1][:, :]).then_inc(set_ev, 1)
            dve.tensor_copy(downT[:, 512:1024], OV[:, :]).then_inc(set_ev, 1)
            dve.tensor_copy(keysT, A[:, :]).then_inc(set_ev, 1)
            dve.wait_ge(set_mm, 1)
            dve.tensor_copy(simW[:, :, :, :].rearrange("p s h k -> p (s h k)"), G[0][:, :]).then_inc(set_w, 1)

            def inverse_root(x, y, t, steps, b, n):
                dve.wait_ge(steps.sem, steps.value(b, n))
                yb = y.bitcast(i32)
                dve.tensor_scalar(yb, x.bitcast(i32), 1, None, ALU.logical_shift_right).then_inc(steps.sem, 1)
                dve.wait_ge(steps.sem, steps.value(b, n + 1))
                dve.tensor_scalar(yb, yb, -1.0, float(0x5F3759DF), ALU.mult, ALU.add).then_inc(steps.sem, 1)
                for k in range(n + 2, n + ROOT_STEPS, 3):
                    dve.wait_ge(steps.sem, steps.value(b, k))
                    dve.tensor_tensor(t, x, y, ALU.mult).then_inc(steps.sem, 1)
                    dve.wait_ge(steps.sem, steps.value(b, k + 1))
                    dve.scalar_tensor_tensor(t, t, -0.5, y, ALU.mult, ALU.mult).then_inc(steps.sem, 1)
                    dve.wait_ge(steps.sem, steps.value(b, k + 2))
                    dve.scalar_tensor_tensor(y, t, 1.5, y, ALU.add, ALU.mult).then_inc(steps.sem, 1)

            def normalise(b, half):
                n = half * (1 + ROOT_STEPS)
                groups = lambda a: a[:, :, :, :, :].rearrange("p s t h d -> p (s t h) d")
                dve.wait_ge(sq_done.sem, sq_done.value(b, 2 * half + 2))
                dve.tensor_reduce(qk_ms[:, :], groups(qk_a), AX.X, ALU.add).then_inc(ms_done.sem, 1)
                dve.wait_ge(ms_done.sem, ms_done.value(b, half + 1))
                dve.tensor_scalar(qk_ms[:, :], qk_ms[:, :], HD * RMS_EPS, None, ALU.add).then_inc(qroot.sem, 1)
                inverse_root(qk_ms[:, :], qk_rs[:, :], qk_t[:, :], qroot, b, n + 1)
                dve.wait_ge(qroot.sem, qroot.value(b, n + 1 + ROOT_STEPS))
                dve.tensor_tensor(groups(qk_n), groups(qk_n), qk_rs[:, :].unsqueeze(2).to_broadcast([P, 64, HD]),
                                  ALU.mult).then_inc(qn_done.sem, 1)

            def shift_by_maxima(b):
                for n in range(NT * NH):
                    t, h = n // NH, n % NH
                    dve.wait_ge(peak_ready.sem, peak_ready.value(b, n + 1))
                    dve.tensor_reduce(peak[:, t, h:h + 1], A[:, 0:(t + 1) * P], AX.X, ALU.max)\
                        .then_inc(peak_done.sem, 1)
                dve.wait_ge(peak_done.sem, peak_done.value(b, NT * NH))
                dve.wait_ge(stack_done.sem, stack_done.value(b, 2))
                dve.memset(shift, 0.0).then_inc(shift_steps.sem, 1)
                for t in range(NT):
                    dve.wait_ge(shift_steps.sem, shift_steps.value(b, 1 + 4 * t))
                    if t:
                        dve.wait_ge(shift_turned.sem, shift_turned.value(b, t))
                    first, second, third = (shift[:, :, SLOTS - 2, i] for i in range(3))
                    dve.tensor_scalar(first, peak[:, t, :], -1.0, None, ALU.mult).then_inc(shift_steps.sem, 1)
                    dve.wait_ge(shift_steps.sem, shift_steps.value(b, 2 + 4 * t))
                    dve.scalar_tensor_tensor(peak_rest[:, t, :], peak[:, t, :], -1.0, first, ALU.mult,
                                             ALU.subtract).then_inc(shift_steps.sem, 1)
                    dve.wait_ge(shift_steps.sem, shift_steps.value(b, 3 + 4 * t))
                    dve.tensor_copy(second, peak_rest[:, t, :]).then_inc(shift_steps.sem, 1)
                    dve.wait_ge(shift_steps.sem, shift_steps.value(b, 4 + 4 * t))
                    dve.tensor_tensor(third, peak_rest[:, t, :], second, ALU.subtract)\
                        .then_inc(shift_steps.sem, 1)
                    dve.wait_ge(shift_turned.sem, shift_turned.value(b, t + 1))
                    qt = qT[:, :, t * P:(t + 1) * P]
                    dve.tensor_tensor(qt, qt, A_b, ALU.add).then_inc(shift_added.sem, 1)

            def normalise_o(b, g):
                if g == 0:
                    dve.wait_ge(out_stored.sem, out_stored.value(b, -16))
                dve.wait_ge(a_ready.sem, a_filled(b, f"o{g}"))
                heads = A[:, :].rearrange("p (t h c) -> p t h c", t=NT, h=4)
                dve.reciprocal(rden[:, :, :], heads[:, :, :, HD]).then_inc(rden_done.sem, 1)
                dve.wait_ge(rden_done.sem, rden_done.value(b, g + 1))
                dve.tensor_tensor(o[:, :, 4 * g:4 * g + 4, :], heads[:, :, :, 0:HD],
                                  rden[:, :, :].unsqueeze(3).to_broadcast([P, NT, 4, HD]), ALU.mult)\
                    .then_inc(o_done.sem, 1)

            def moments(src, i, steps, b):
                dve.wait_ge(steps.sem, steps.value(b, 1))
                for t in range(NT):
                    last = dve.bn_stats(stats[:, t, :], src[:, t, :])
                last.then_inc(steps.sem, 1)
                dve.wait_ge(steps.sem, steps.value(b, 2))
                pass_wait(dve)
                for t in range(NT):
                    last = dve.bn_aggr(mv[i][:, t, :], stats[:, t, :])
                last.then_inc(steps.sem, 1)
                dve.wait_ge(steps.sem, steps.value(b, 3))

            def norm1(b):
                dve.wait_ge(a_ready.sem, a_filled(b, "proj"))
                dve.wait_ge(xr_loaded.sem, xr_loaded.value(b, 16))
                dve.tensor_tensor(r1[:, :, :].rearrange("p t d -> p (t d)"), A[:, :],
                                  xr[:, :, :].rearrange("p t d -> p (t d)"), ALU.add).then_inc(ln1.sem, 1)
                moments(r1, 0, ln1, b)
                dve.tensor_scalar(var[0][:, 0, :], mv[0][:, :, 1], LN_EPS, None, ALU.add)
                dve.tensor_scalar(var[0][:, 1, :], mv[0][:, :, 1], 1.0 + RMS_EPS, RMS_EPS * LN_EPS,
                                  ALU.mult, ALU.add).then_inc(ln1.sem, 1)
                inverse_root(var[0][:, :, :], rs[0][:, :, :], rs_t[:, :, :], ln1, b, 4)
                dve.wait_ge(ln1.sem, ln1.value(b, 4 + ROOT_STEPS))
                for t in range(NT):
                    last = dve.tensor_scalar(yi[:, t, :], r1[:, t, :], mv[0][:, t, 0:1], rs[0][:, 1, t:t + 1],
                                             ALU.subtract, ALU.mult)
                last.then_inc(yi_done.sem, 1)

            def norm1_rows(b):
                for t in range(NT):
                    last = dve.tensor_scalar(y[:, t, :], r1[:, t, :], mv[0][:, t, 0:1], rs[0][:, 0, t:t + 1],
                                             ALU.subtract, ALU.mult)
                last.then_inc(ln1.sem, 1)

            def norm2(b):
                dve.wait_ge(ffn_ready.sem, ffn_ready.value(b, 1))
                dve.wait_ge(out_stored.sem, out_stored.value(b, 0))
                dve.wait_ge(ln1.sem, ln1.value(b, ln1.per_batch))
                dve.tensor_tensor(r2[:, :, :].rearrange("p t d -> p (t d)"), OV[:, :],
                                  y[:, :, :].rearrange("p t d -> p (t d)"), ALU.add).then_inc(ln2.sem, 1)
                moments(r2, 1, ln2, b)
                dve.tensor_scalar(var[1][:, 0, :], mv[1][:, :, 1], LN_EPS, None, ALU.add).then_inc(ln2.sem, 1)
                inverse_root(var[1][:, 0, :], rs[1][:, 0, :], rs_t[:, 0, :], ln2, b, 4)
                dve.wait_ge(ln2.sem, ln2.value(b, 4 + ROOT_STEPS))
                for t in range(NT):
                    last = dve.tensor_scalar(r2[:, t, :], r2[:, t, :], mv[1][:, t, 0:1], rs[1][:, 0, t:t + 1],
                                             ALU.subtract, ALU.mult)
                last.then_inc(out_ready.sem, 1)

            def top_keys(b, t):
                dve.wait_ge(sims_done.sem, sims_done.value(b, t + 1))
                pass_wait(dve)
                for s in range(2):
                    for h in range(H):
                        last = dve.max(out=topv[:, t, s, h, :], in_=sims[:, t % 2, s, h, :])
                last.then_inc(topv_done.sem, 1)
                dve.wait_ge(topv_done.sem, topv_done.value(b, t + 1))
                pass_wait(dve)
                for s in range(2):
                    for h in range(H):
                        last = dve.max_index(topi[:, t, s, h, :], topv[:, t, s, h, :], sims[:, t % 2, s, h, :])
                last.then_inc(top1_done.sem, 1)

            def top_pairs(b, t):
                dve.wait_ge(cand_done.sem, cand_done.value(b, t + 1))
                pass_wait(dve)
                for h in range(H):
                    last = dve.max(out=fsel[:, t, h, :], in_=candv[:, t % 2, h, :])
                last.then_inc(fsel_done.sem, 1)
                dve.wait_ge(fsel_done.sem, fsel_done.value(b, t + 1))
                pass_wait(dve)
                for h in range(H):
                    last = dve.max_index(psel[:, t % 2, h, :], fsel[:, t, h, :], candv[:, t % 2, h, :])
                last.then_inc(top2_done.sem, 1)
                dve.wait_ge(top2_done.sem, top2_done.value(b, t + 1))
                dims = [P, H, NCAND, TOPK]
                dve.tensor_tensor(gat[:, t % 2], psel[:, t % 2].unsqueeze(2).to_broadcast(dims),
                                  cand_no[:, :, :].unsqueeze(1).to_broadcast(dims), ALU.is_equal)\
                    .then_inc(hotc_done.sem, 1)

            def selected(b, t):
                dve.wait_ge(gat_done.sem, gat_done.value(b, 2 * t + 2))
                dve.tensor_reduce(esel[:, t, :].rearrange("p (h k) -> p h k", h=H),
                                  gat[:, t % 2, :, 0:10, :].rearrange("p h c k -> p h k c"), AX.X, ALU.add).then_inc(esel_done.sem, 1)

            def decode(b):
                bank = bank_f("sel")
                flat = lambda a: a.rearrange("p a t -> p (a t)")
                e, w = bank[:, 0:2 * P], bank[:, 2 * P:4 * P]
                w0, w1, w2 = (flat(wpart[:, i]) for i in range(3))
                dve.wait_ge(f_ready.sem, f_filled(b, "sel"))
                dve.tensor_copy(flat(eint[:, :, :]), e)
                dve.tensor_scalar(w0, w, 0.0, None, ALU.max).then_inc(dec.sem, 1)
                dve.wait_ge(dec.sem, dec.value(b, 1))
                dve.tensor_scalar(flat(elo[:, :, :]), flat(eint[:, :, :]), P - 1, None, ALU.bitwise_and)
                dve.tensor_scalar(flat(ehi[:, :, :]), flat(eint[:, :, :]), NEXP - P, None, ALU.bitwise_and)
                dve.scalar_tensor_tensor(flat(wrest[:, :, :]), w, 0.0, w0, ALU.max, ALU.subtract)\
                    .then_inc(dec.sem, 1)
                dve.wait_ge(dec.sem, dec.value(b, 2))
                dve.tensor_copy(w1, flat(wrest[:, :, :])).then_inc(dec.sem, 1)
                dve.wait_ge(dec.sem, dec.value(b, 3))
                dve.tensor_tensor(w2, flat(wrest[:, :, :]), w1, ALU.subtract).then_inc(dec.sem, 1)

            def one_hots(b, los):
                dve.wait_ge(dec.sem, dec.value(b, 4))
                for lo in los:
                    last = dve.tensor_scalar(onehot[:, lo, :, :], elo[:, :, :], float(lo), None, ALU.is_equal)

            def hi_one_hots(b):
                for hi in range(NHI):
                    last = dve.tensor_scalar(hot_hi[:, hi, :], ehi[:, :, :].rearrange("p a t -> p (a t)"),
                                             float(hi * P), None, ALU.is_equal)
                last.then_inc(hot_done.sem, 1)

            def weighted_one_hots(b, pair):
                dve.wait_ge(hot_done.sem, hot_done.value(b, 1))
                if pair == 1:
                    dve.wait_ge(g_ready.sem, g_ready.value(b, 4))
                for part in range(3):
                    for i in range(2):
                        rows = slice(64 * i, 64 * i + 64)
                        w = wpart[rows, part, pair, :].unsqueeze(1).to_broadcast([64, NHI, P])
                        last = dve.tensor_tensor(whot[rows, part, i], hot_hi[rows, :, pair * P:pair * P + P], w,
                                                 ALU.mult)
                last.then_inc(hot_done.sem, 1)

            def apply_weights(b, chunk):
                if chunk == 0:
                    dve.wait_ge(hid_done.sem, hid_done.value(b, NHI))
                dve.wait_ge(g_ready.sem, g_ready.value(b, chunk + 1))
                pair, t0 = chunk // 4, chunk % 4 * 32
                h = hid[:, :, :].rearrange("p c (a s t) -> p a s c t", a=2, s=2)[:, pair, :, :, t0:t0 + 32]
                g = G[chunk % 2][:, :].rearrange("p (t s c) -> p s c t", s=2, c=NHI)
                dve.tensor_tensor(h, g, h, ALU.mult).then_inc(g_free.sem, 1)

            def iteration(b, late, nxt):
                if b is not None:
                    normalise_o(b, 0)
                if late is not None:
                    one_hots(late, range(0, 40))
                if b is not None:
                    normalise_o(b, 1)
                if late is not None:
                    one_hots(late, range(40, 80))
                if b is not None:
                    normalise_o(b, 2)
                if late is not None:
                    one_hots(late, range(80, P))
                    hi_one_hots(late)
                    weighted_one_hots(late, 0)
                if b is not None:
                    normalise_o(b, 3)
                    norm1(b)
                    top_keys(b, 0)
                if late is not None:
                    apply_weights(late, 0)
                if nxt is not None:
                    normalise(nxt, 0)
                if b is not None:
                    top_keys(b, 1)
                if late is not None:
                    apply_weights(late, 1)
                    apply_weights(late, 2)
                if b is not None:
                    top_keys(b, 2)
                if late is not None:
                    apply_weights(late, 3)
                    weighted_one_hots(late, 1)
                if b is not None:
                    top_pairs(b, 0)
                    top_keys(b, 3)
                if nxt is not None:
                    normalise(nxt, 1)
                if late is not None:
                    apply_weights(late, 4)
                if b is not None:
                    top_pairs(b, 1)
                    selected(b, 0)
                if late is not None:
                    apply_weights(late, 5)
                    apply_weights(late, 6)
                if b is not None:
                    top_pairs(b, 2)
                    selected(b, 1)
                if late is not None:
                    apply_weights(late, 7)
                if nxt is not None:
                    with dve.If(far_scores != 0):
                        shift_by_maxima(nxt)
                if b is not None:
                    top_pairs(b, 3)
                    selected(b, 2)
                    selected(b, 3)
                if late is not None:
                    norm2(late)
                if b is not None:
                    norm1_rows(b)
                    decode(b)

            iteration(None, None, 0)
            iteration(0, None, 1)
            with dve.Fori(1, BATCH - 1) as b:
                iteration(b, b - 1, b + 1)
            iteration(BATCH - 1, BATCH - 2, None)
            iteration(None, BATCH - 1, None)


_INS = ["L0_attn_x", "L0_attn_w_qkv", "L0_attn_w_proj", "L0_attn_q_norm_w", "L0_attn_k_norm_w", "L0_ffn_w_q",
        "L0_ffn_keys", "L0_ffn_expert_down", "L0_ffn_expert_up", "L0_ffn_norm_w"]


def rope_constants(seq_len, head_dim, theta):
    import numpy as np
    freqs = theta ** (-np.arange(0, head_dim, 2, dtype=np.float32) / head_dim)
    ang = np.arange(seq_len, dtype=np.float32)[:, None] * freqs.astype(np.float32)[None, :]
    return np.stack([np.cos(ang), np.sin(ang)], axis=1).astype(np.float32)


def kernel(**inputs):
    import numpy as np
    import concourse.bacc as bacc
    from concourse import mybir
    from concourse.bass_utils import run_bass_kernel_spmd

    nc = bacc.Bacc("TRN2", target_bir_lowering=False, num_devices=1)
    arrays = {f"in_{n}": np.ascontiguousarray(inputs[n]) for n in _INS}
    arrays["in_rope"] = rope_constants(inputs["L0_attn_x"].shape[1], inputs["L0_attn_q_norm_w"].shape[0], 32.0)
    args = [nc.dram_tensor(n, a.shape, mybir.dt.from_np(a.dtype), kind="ExternalInput").ap()
            for n, a in arrays.items()]
    out = nc.dram_tensor("out", inputs["L0_attn_x"].shape, mybir.dt.float32, kind="ExternalOutput").ap()
    attention_then_peer_layer(nc, *args, out)
    return run_bass_kernel_spmd(nc, [arrays], core_ids=[0]).results[0]["out"]
```

```python
import concourse.bass as bass
from concourse import mybir
from contextlib import ExitStack
from itertools import islice


class Signal:

    def __init__(self, sem, per_batch, seed=0):
        self.sem, self.per_batch, self.seed = sem, per_batch, seed

    def value(self, b, n):
        assert self.seed + n >= 1 or (isinstance(b, int) and b * self.per_batch + self.seed + n >= 1)
        return b * self.per_batch + (self.seed + n)


def attention_then_peer_layer(nc, x, w_qkv, w_proj, q_norm_w, k_norm_w, w_q, keys, expert_down, expert_up,
                              norm_w, rope_table, out):
    fp32, bf16, fp16, u16, i32 = (
        mybir.dt.float32, mybir.dt.bfloat16, mybir.dt.float16, mybir.dt.uint16, mybir.dt.int32)
    ALU, ACT, AX = mybir.AluOpType, mybir.ActivationFunctionType, mybir.AxisListType

    P = 128
    BATCH, T, D = x.shape
    NT = T // P
    NH, HD = 16, 8
    NPAIR = NH // 2
    SLOTS = 8
    SCALE = float(HD) ** -0.5
    H, NK, TOPK = keys.shape[0], keys.shape[1], 8
    NEXP = expert_down.shape[0]
    NHI = NEXP // P
    NCAND = 20
    SAFE_SCORE = 64.0
    LN_EPS, RMS_EPS = 1e-5, 1e-6
    NEG = -1e30

    KC_AT = [0, 512, 1024, 896]
    PCOLS = 1280
    UNITS = 5 * 2
    NG = NH // 4

    ctx = ExitStack()
    with ctx:
        def sb(name, shape, dt):
            return ctx.enter_context(nc.sbuf_tensor(name, shape, dt))

        def pb(name):
            return ctx.enter_context(nc.psum_tensor(name, [P, 512], fp32))

        def sem(name):
            return ctx.enter_context(nc.semaphore(name))

        ident = sb("ident", [P, P], fp32)
        ident_b = sb("ident_b", [P, P], bf16)
        causal = sb("causal", [P, P], bf16)
        cand_no = sb("cand_no", [P, NCAND, TOPK], u16)
        wqkvT = sb("wqkvT", [P, 3 * D], fp32)
        wprojT = sb("wprojT", [P, D], fp32)
        simW = sb("simW", [P, 2, H, NK], fp32)
        downT = sb("downT", [P, NEXP], fp32)
        up = sb("up", [P, NHI, D], fp32)
        normw = sb("normw", [P, 1], fp32)
        far = sb("far", [P, 1], i32)
        cosw = sb("cosw", [P, NT, 2, HD], fp32)
        sinw = sb("sinw", [P, NT, 2, HD], fp32)
        spare_out = sb("spare_out", [1, 2], fp32)
        xa = sb("xa", [P, NT, D], fp32)
        xr = sb("xr", [P, NT, D], fp32)
        xT = sb("xT", [P, T], fp32)
        qk_a = sb("qk_a", [P, 2, 2, NH, HD], fp32)
        qk_n = sb("qk_n", [P, 2, 2, NH, HD], fp32)
        qk_u = sb("qk_u", [P, 2, 2, NH, HD], fp32)
        qk_ms = sb("qk_ms", [P, 64 + NT], fp32)
        qk_rs = sb("qk_rs", [P, 64 + NT], fp32)
        qk_t = sb("qk_t", [P, 64 + NT], fp32)
        stack = sb("stack", [P, 2, 2, NH, SLOTS, HD], bf16)
        qT = sb("qT", [P, NPAIR, T], bf16)
        kT = [sb("kT_even", [P, NPAIR, T], bf16), sb("kT_odd", [P, NPAIR, T], bf16)]
        vp = sb("vp", [P, NT, NH, HD + 1], fp32)
        prob = sb("prob", [P, 4, PCOLS], fp32)
        xn = sb("xn", [P, T], fp32)
        rden = sb("rden", [P, NT, 4], fp32)
        r2 = sb("r2", [P, NT, D], fp32)
        o = r2[:, :, :].rearrange("p t (h d) -> p t h d", h=NH)
        r1 = xr
        stats = sb("stats", [P, NT, 6], fp32)
        mv = [sb("mv1", [P, NT, 2], fp32), sb("mv2", [P, NT, 2], fp32)]
        var = sb("var", [P, 2, NT], fp32)
        rs = sb("rs", [P, 2, NT], fp32)
        rs_t = sb("rs_t", [P, 2, NT], fp32)
        y_new = sb("y_new", [P, NT, D], fp32)
        y = sb("y", [P, NT, D], fp32)
        yi = sb("yi", [P, NT, D], fp32)
        oT = oTn = yi[:, :, :].rearrange("p t d -> p (t d)")
        sims = sb("sims", [P, 2, 2, H, NK], fp32)
        topv = sb("topv", [P, NT, 2, H, TOPK], fp32)
        topi = sb("topi", [P, NT, 2, H, TOPK], u16)
        i12 = sb("i12", [P, 2, H, TOPK], fp16)
        candv = sb("candv", [P, 2, H, NCAND], fp32)
        cande = sb("cande", [P, 2, H, NCAND], fp16)
        fsel = sb("fsel", [P, NT, H, TOPK], fp32)
        psel = sb("psel", [P, 2, H, TOPK], u16)
        gat = sb("gat", [P, 2, H, NCAND, TOPK], fp16)
        qk_r = gat[:, :, :, :, :].rearrange("p a h c k -> p (a h c k)").bitcast(fp32)[:, 0:512]\
            .rearrange("p (s t h d) -> p s t h d", s=2, t=2, h=NH)
        esel = sb("esel", [P, NT, H * TOPK], fp32)
        eint = sb("eint", [P, 2, P], u16)
        elo = sb("elo", [P, 2, P], u16)
        ehi = sb("ehi", [P, 2, P], u16)
        wpart = sb("wpart", [P, 3, 2, P], bf16)
        wrest = sb("wrest", [P, 2, P], fp32)
        onehot = sb("onehot", [P, P, 2, P], bf16)
        hot_hi = sb("hot_hi", [P, NHI, 2 * P], bf16)
        whot = sb("whot", [P, 3, 2, NHI, P], bf16)
        hid = sb("hid", [P, NHI, T], fp32)

        tmp = onehot[:, :, :, :].rearrange("p a b c -> p (a b c)").bitcast(fp32)
        wq_raw = tmp[:, 0:2048].rearrange("p (g d) -> p g d", g=16)
        keys_raw = tmp[:, 2048:2560].rearrange("p (c s d) -> p c s d", c=2, s=2)
        keysT = tmp[:, 2560:3072]
        wqkv_raw = tmp[:, 3072:3456].rearrange("p (g d) -> p g d", g=3)
        wproj_raw = tmp[:, 3456:3584]
        down_raw = tmp[:, 3584:4608].rearrange("p (g d) -> p g d", g=8)
        rope = tmp[:, 4608:4640].rearrange("p (t c d) -> p t c d", t=NT, c=2)
        qkw = tmp[:, 4640:4656].rearrange("p (s d) -> p s d", s=2)

        qkw_sq = tmp[:, 4656:4672].rearrange("p (s d) -> p s d", s=2)
        pair_sq = tmp[:, 4672:4680].rearrange("p (s d) -> p s d", s=2)
        score_sq = tmp[:, 4680:4684]
        most_sq = tmp[:, 4684:4685]
        peak, peak_rest = (x[:, 0:64].rearrange("p (t h) -> p t h", t=NT) for x in (qk_t, qk_ms))
        shift = qk_u[:, :, :, :, :].rearrange("p s t h d -> p (s t h d)").bitcast(bf16)\
            .rearrange("p (h c d) -> p h c d", h=NH, c=SLOTS)

        S = [pb("S0"), pb("S1")]
        OV = pb("OV")
        A = pb("A")
        F = [pb("F0"), pb("F1")]
        G = [pb("G0"), pb("G1")]

        def stacked(bank):
            return bank[:, :].bitcast(bf16).rearrange("p (j t) -> p j t", j=NPAIR)

        w_loaded, const_done, zero_done = sem("w_loaded"), sem("const_done"), sem("zero_done")
        set_tr, set_ev, set_mm, set_w = sem("set_tr"), sem("set_ev"), sem("set_mm"), sem("set_w")

        waits_passed = sem("waits_passed")

        ROOT_STEPS = 11

        def signal(name, per_batch, seed=0):
            return Signal(sem(name), per_batch, seed)

        xa_loaded = signal("xa_loaded", 16)
        xr_loaded = signal("xr_loaded", 16)
        out_stored = signal("out_stored", 16, 48)
        a_ready = signal("a_ready", 6)
        c_ready = signal("c_ready", 13)
        xT_done = signal("xT_done", 1)
        sq_done = signal("sq_done", NT)
        v_done = signal("v_done", NT)
        ms_done = signal("ms_done", 2)
        qroot = signal("qroot", 2 * (1 + ROOT_STEPS))
        qn_done = signal("qn_done", 2)
        rope_done = signal("rope_done", 8)
        rot_done = signal("rot_done", 4, 1)
        first_done = signal("first_done", 2)
        rest_done = signal("rest_done", 2)
        second_done = signal("second_done", 2)
        stack_done = signal("stack_done", 2, 1)
        qT_done = signal("qT_done", NT)
        kT_done = signal("kT_done", NT)
        s_ready = signal("s_ready", NG * UNITS)
        exp_done = signal("exp_done", NG * UNITS, 2)
        pv_done = signal("pv_done", NG, 1)
        oT_done = signal("oT_done", NG, 1)
        rden_done = signal("rden_done", NG)
        o_done = signal("o_done", NG)
        oTn_done = signal("oTn_done", 1)
        ln1 = signal("ln1", 5 + ROOT_STEPS, 5 + ROOT_STEPS)
        yi_done = signal("yi_done", 1)
        f_ready = signal("f_ready", 14)
        xn_done = signal("xn_done", 1)
        sims_done = signal("sims_done", NT, 1)
        topv_done = signal("topv_done", NT)
        top1_done = signal("top1_done", NT, 2)
        i12_done = signal("i12_done", NT)
        cand_done = signal("cand_done", NT, 1)
        fsel_done = signal("fsel_done", NT)
        top2_done = signal("top2_done", NT)
        hotc_done = signal("hotc_done", NT)
        gat_done = signal("gat_done", 2 * NT)
        esel_done = signal("esel_done", NT)
        hid_done = signal("hid_done", NHI, 2)
        dec = signal("dec", 4, 4)
        hot_done = signal("hot_done", 3)
        g_ready = signal("g_ready", 8)
        g_free = signal("g_free", 8, 2)
        ffn_ready = signal("ffn_ready", 1)
        ln2 = signal("ln2", 4, 3 * 4)
        root_alone = signal("root_alone", ROOT_STEPS)
        kept = signal("kept", 1, 1)
        out_ready = signal("out_ready", 1)
        seeded = [out_stored, sims_done, hid_done, kept, rot_done, stack_done, exp_done, pv_done, oT_done, ln1, dec, ln2, cand_done, top1_done, g_free]

        peak_ready = signal("peak_ready", NT * NH)
        peak_done = signal("peak_done", NT * NH)
        shift_steps = signal("shift_steps", 1 + 4 * NT)
        shift_turned = signal("shift_turned", NT)
        shift_added = signal("shift_added", NT)
        bound_steps = sem("bound_steps")

        A_USES = [(f"o{g}", [(o_done, g + 1)]) for g in range(NG)]
        A_USES += [("oTn", [(oTn_done, 1)]), ("proj", [(ln1, 1)])]
        C_USES = [("xT", [(xT_done, 1)])]
        C_USES += [(f"qkv{t}", [(v_done, t + 1)]) for t in range(NT)]
        for t in range(NT):
            C_USES += [(f"Q{t}", [(qT_done, t + 1)]), (f"K{t}", [(kT_done, t + 1)])]
        F_USES = [("xn", [(xn_done, 1)])]
        F_USES += [(f"sims{t}", [(sims_done, t + 1)]) for t in range(NT)]
        F_USES += [("sel", [(dec, 2)])]
        F_USES += [(f"hid{c}", [(hid_done, c + 1)]) for c in range(NHI)]

        def pass_wait(eng):
            eng.sem_inc(waits_passed, 1)

        def number(uses, use):
            return [name for name, _ in uses].index(use)

        def wait_read(eng, b, uses, i):
            for s, n in uses[i][1]:
                eng.wait_ge(s.sem, s.value(b, n - s.per_batch if i < 0 else n))

        def a_filled(b, use):
            return a_ready.value(b, number(A_USES, use) + 1)

        def wait_a_empty(eng, b, use):
            wait_read(eng, b, A_USES, number(A_USES, use) - 1)

        def bank_c(use):
            return S[number(C_USES, use) % 2]

        def c_filled(b, use):
            return c_ready.value(b, number(C_USES, use) + 1)

        def wait_c_empty(eng, b, use):
            i = number(C_USES, use) - 2
            if i < 0:
                eng.wait_ge(exp_done.sem, exp_done.value(b, 0))
            else:
                wait_read(eng, b, C_USES, i)

        def bank_f(use):
            return F[number(F_USES, use) % 2]

        def f_filled(b, use):
            return f_ready.value(b, number(F_USES, use) + 1)

        def wait_f_empty(eng, b, use):
            wait_read(eng, b, F_USES, number(F_USES, use) - 2)

        SCORES = [[(0, 0, 0)], [(0, 1, 0), (0, 3, 384)], [(0, 2, 0), (1, 2, 256)],
                  [(1, 0, 0)], [(1, 1, 0), (1, 3, 384)]]

        SIMS_UNIT = 4
        SELECTION_STEP = 34
        WEIGHT_STEPS = list(range(1, 9)) + list(range(13, 29))

        block = ctx.enter_context(nc.Block())

        @block.sync
        def _(sp):
            loads = [
                (wq_raw, w_q.rearrange("(g p) d -> p g d", p=P)),
                (keys_raw, keys.rearrange("(c h) k s d -> (h k) c s d", c=2)),
                (wqkv_raw, w_qkv.rearrange("(g p) d -> p g d", p=P)),
                (wproj_raw, w_proj),
                (down_raw, expert_down.rearrange("(g p) d -> p g d", p=P)),
                (up[:, :, :], expert_up.rearrange("(g p) d -> p g d", p=P)),
                (normw[:, :], norm_w.rearrange("(p a) -> p a", a=1)),
                (qkw[:, 0, :], q_norm_w.rearrange("(a n) -> a n", a=1).to_broadcast([P, HD])),
                (qkw[:, 1, :], k_norm_w.rearrange("(a n) -> a n", a=1).to_broadcast([P, HD])),
                (rope[:, :, :, :], rope_table.rearrange("(t p) c d -> p t c d", p=P)),
            ]
            for dst, src in loads:
                sp.dma_start(dst, src).then_inc(w_loaded, 16)

            def load_xa(b):
                sp.dma_start(xa[:, :, :], x[b].rearrange("(t p) d -> p t d", p=P)).then_inc(xa_loaded.sem, 16)

            def load_xr(b):
                sp.dma_start(xr[:, :, :], x[b].rearrange("(t p) d -> p t d", p=P)).then_inc(xr_loaded.sem, 16)

            def store(b):
                sp.wait_ge(out_ready.sem, out_ready.value(b, 1))
                sp.dma_start(out[b].rearrange("(t p) d -> p t d", p=P), r2[:, :, :]).then_inc(out_stored.sem, 16)

            def next_xa(b):
                sp.wait_ge(c_ready.sem, c_filled(b, "xT"))
                load_xa(b + 1)

            def next_xr(b):
                sp.wait_ge(ln1.sem, ln1.value(b, ln1.per_batch))
                load_xr(b + 1)

            load_xa(0)
            load_xr(0)
            next_xa(0)
            for b in (1, 2):
                next_xa(b)
                next_xr(b - 1)
            with sp.Fori(3, BATCH - 1) as b:
                next_xa(b)
                store(b - 3)
                next_xr(b - 1)
            store(BATCH - 4)
            next_xr(BATCH - 2)
            for b in range(BATCH - 3, BATCH):
                store(b)
            sp.wait_ge(out_stored.sem, out_stored.value(BATCH - 1, 16))

        @block.gpsimd
        def _(pool):
            pool.memset(ident[:, :], 0.0).then_inc(zero_done, 1)
            pool.memset(ident_b[:, :], 0.0).then_inc(zero_done, 1)
            pool.memset(causal[:, :], 0.0).then_inc(zero_done, 1)
            pool.wait_ge(zero_done, 3)
            for m in (ident, ident_b):
                pool.affine_select(out=m[:, :], in_=m[:, :], compare_op=ALU.not_equal, fill=1.0, base=0,
                                   pattern=[[-1, P]], channel_multiplier=1).then_inc(const_done, 1)
            pool.affine_select(out=causal[:, :], in_=causal[:, :], compare_op=ALU.is_ge, fill=NEG, base=0,
                               pattern=[[1, P]], channel_multiplier=-1).then_inc(const_done, 1)
            pool.iota(cand_no[:, :, :], pattern=[[1, NCAND], [0, TOPK]], base=0, channel_multiplier=0).then_inc(const_done, 1)
            pool.wait_ge(const_done, 4)

            def rotate(b, half):
                pool.wait_ge(qn_done.sem, qn_done.value(b, half + 1))
                pool.wait_ge(stack_done.sem, stack_done.value(b, half))
                for i in range(2):
                    for dst, tab in ((qk_a, cosw), (qk_u, sinw)):
                        w = tab[:, 2 * half + i].unsqueeze(2).to_broadcast([P, 2, NH, HD])
                        pool.tensor_tensor(dst[:, :, i], qk_n[:, :, i], w, ALU.mult).then_inc(rope_done.sem, 1)
                pool.wait_ge(rope_done.sem, rope_done.value(b, 4 * half + 4))
                a, u, r = (x[:, :, :, :, :].rearrange("p s t h d -> p (s t h) d") for x in (qk_a, qk_u, qk_r))
                pool.tensor_tensor(r[:, :, 0:4], a[:, :, 0:4], u[:, :, 4:8], ALU.subtract).then_inc(rot_done.sem, 1)
                pool.tensor_tensor(r[:, :, 4:8], a[:, :, 4:8], u[:, :, 0:4], ALU.add).then_inc(rot_done.sem, 1)

            def split(b, half):
                st = stack[:, :, :, :, :, :].rearrange("p s t h c d -> p (s t h) c d")
                u, r = (x[:, :, :, :, :].rearrange("p s t h d -> p (s t h) d") for x in (qk_u, qk_r))
                pool.wait_ge(first_done.sem, first_done.value(b, half + 1))
                pool.tensor_tensor(u, r, st[:, :, 2, :], ALU.subtract).then_inc(rest_done.sem, 1)
                pool.wait_ge(second_done.sem, second_done.value(b, half + 1))
                pool.tensor_tensor(st[:, 0:32, 4, :], u[:, 0:32], st[:, 0:32, 5, :], ALU.subtract)
                pool.tensor_tensor(st[:, 32:64, 0, :], u[:, 32:64], st[:, 32:64, 5, :], ALU.subtract)\
                    .then_inc(stack_done.sem, 1)

            def candidates(b, t):
                pool.wait_ge(top1_done.sem, top1_done.value(b, t + 1))
                pool.wait_ge(cand_done.sem, cand_done.value(b, t))
                pass_wait(pool)
                for side, scale in enumerate((NK, 1)):
                    last = pool.tensor_scalar(i12[:, side], topi[:, t, side], float(scale), None, ALU.mult)
                last.then_inc(i12_done.sem, 1)
                pool.wait_ge(i12_done.sem, i12_done.value(b, t + 1))
                last = None
                for dst, one, two in ((candv, topv[:, t, 0], topv[:, t, 1]), (cande, i12[:, 0], i12[:, 1])):
                    c = dst[:, t % 2]
                    pool.tensor_tensor(c[:, :, 0:8], one[:, :, 0:1].to_broadcast([P, H, 8]), two, ALU.add)
                    pool.tensor_tensor(c[:, :, 8:12], one[:, :, 1:2].to_broadcast([P, H, 4]), two[:, :, 0:4],
                                       ALU.add)
                    pool.tensor_tensor(c[:, :, 12:16].rearrange("p h (a b) -> p h a b", a=2),
                                       one[:, :, 2:4].unsqueeze(3).to_broadcast([P, H, 2, 2]),
                                       two[:, :, 0:2].unsqueeze(2).to_broadcast([P, H, 2, 2]), ALU.add)
                    last = pool.tensor_tensor(c[:, :, 16:20], one[:, :, 4:8],
                                              two[:, :, 0:1].to_broadcast([P, H, 4]), ALU.add)
                last.then_inc(cand_done.sem, 1)

            def gather(b, t):
                pool.wait_ge(hotc_done.sem, hotc_done.value(b, t + 1))
                g = gat[:, t % 2]
                pool.tensor_tensor(g, g, cande[:, t % 2].unsqueeze(3).to_broadcast([P, H, NCAND, TOPK]), ALU.mult)\
                    .then_inc(gat_done.sem, 1)
                pool.wait_ge(gat_done.sem, gat_done.value(b, 2 * t + 1))
                pool.tensor_tensor(g[:, :, 0:10], g[:, :, 0:10], g[:, :, 10:20], ALU.add)\
                    .then_inc(gat_done.sem, 1)

            def keep_rows(b):
                pool.wait_ge(ln1.sem, ln1.value(b, ln1.per_batch))
                pool.wait_ge(ln2.sem, ln2.value(b, 1 - ln2.per_batch))
                pass_wait(pool)
                pool.tensor_copy(y[:, :, :], y_new[:, :, :]).then_inc(kept.sem, 1)

            def iteration(b, late, older, nxt):
                if late is not None:
                    candidates(late, 0)
                    candidates(late, 1)
                    gather(late, 0)
                    candidates(late, 2)
                    gather(late, 1)
                    candidates(late, 3)
                    gather(late, 2)
                    gather(late, 3)
                if nxt is not None:
                    for half in range(2):
                        rotate(nxt, half)
                        split(nxt, half)
                if late is not None:
                    keep_rows(late)

            iteration(None, None, None, 0)
            iteration(0, None, None, 1)
            iteration(1, 0, None, 2)
            with pool.Fori(2, BATCH - 1) as b:
                iteration(b, b - 1, b - 2, b + 1)
            iteration(BATCH - 1, BATCH - 2, BATCH - 3, None)
            iteration(None, BATCH - 1, BATCH - 2, None)
            iteration(None, None, BATCH - 1, None)

        @block.scalar
        def _(act):
            act.wait_ge(w_loaded, 160)
            spare_in = normw[0:1, 0:1]

            def normed(b):
                act.wait_ge(f_ready.sem, f_filled(b, "xn"))
                bank = bank_f("xn")
                act.activation(xn[:, :], bank[:, :], ACT.Copy, scale=normw[:, 0:1]).then_inc(xn_done.sem, 1)

            def similarities(b, t):
                act.wait_ge(f_ready.sem, f_filled(b, f"sims{t}"))
                act.wait_ge(top1_done.sem, top1_done.value(b, t - 1))
                bank = bank_f(f"sims{t}")
                act.activation(sims[:, t % 2].rearrange("p s h k -> p (s h k)"), bank[:, :], ACT.Copy)\
                    .then_inc(sims_done.sem, 1)

            def hidden(b, c):
                act.wait_ge(f_ready.sem, f_filled(b, f"hid{c}"))
                bank = bank_f(f"hid{c}")
                act.activation(hid[:, c, :], bank[:, :], ACT.Gelu).then_inc(hid_done.sem, 1)

            def taken_qkv(b, t):
                act.wait_ge(c_ready.sem, c_filled(b, f"qkv{t}"))
                bank = bank_c(f"qkv{t}")
                act.wait_ge(rot_done.sem, rot_done.value(b, t // 2 * 2))
                sides = bank[:, 0:2 * D].rearrange("p (s h d) -> p s h d", s=2, h=NH)
                act.activation(qk_a[:, :, t % 2], sides, ACT.Square)
                act.activation(qk_n[:, :, t % 2], sides, ACT.Copy).then_inc(sq_done.sem, 1)
                act.activation(vp[:, t, :, 0:HD], bank[:, 2 * D:3 * D].rearrange("p (h d) -> p h d", h=NH), ACT.Copy)\
                    .then_inc(v_done.sem, 1)

            def first_parts(b, half):
                st = stack[:, :, :, :, :, :].rearrange("p s t h c d -> p (s t h) c d")
                r = qk_r[:, :, :, :, :].rearrange("p s t h d -> p (s t h) d").unsqueeze(2)\
                    .to_broadcast([P, 64, 3, HD])
                act.wait_ge(rot_done.sem, rot_done.value(b, 2 * half + 2))
                act.activation(st[:, 0:32, 0:3, :], r[:, 0:32], ACT.Copy)
                act.activation(st[:, 32:64, 2:5, :], r[:, 32:64], ACT.Copy).then_inc(first_done.sem, 1)

            def second_parts(b, half):
                st = stack[:, :, :, :, :, :].rearrange("p s t h c d -> p (s t h) c d")
                u = qk_u[:, :, :, :, :].rearrange("p s t h d -> p (s t h) d").unsqueeze(2)\
                    .to_broadcast([P, 64, 2, HD])
                act.wait_ge(rest_done.sem, rest_done.value(b, half + 1))
                act.activation(st[:, 0:32, 3:6:2, :], u[:, 0:32], ACT.Copy)
                act.activation(st[:, 32:64, 1:6:4, :], u[:, 32:64], ACT.Copy).then_inc(second_done.sem, 1)

            def transposed(b, t):
                act.wait_ge(c_ready.sem, c_filled(b, f"Q{t}"))
                act.activation(qT[:, :, t * P:(t + 1) * P], stacked(bank_c(f"Q{t}")), ACT.Copy)\
                    .then_inc(qT_done.sem, 1)
                act.wait_ge(c_ready.sem, c_filled(b, f"K{t}"))
                src = stacked(bank_c(f"K{t}"))
                act.activation(kT[0][0:64, :, t * P:(t + 1) * P], src[0:64], ACT.Copy)
                act.activation(kT[1][64:128, :, t * P:(t + 1) * P], src[64:128], ACT.Copy).then_inc(kT_done.sem, 1)

            def exps(b, g, units):
                act.wait_ge(pv_done.sem, pv_done.value(b, g))
                for u in units:
                    n = g * UNITS + u
                    act.wait_ge(s_ready.sem, s_ready.value(b, n + 1))
                    h = 2 * (u // 5)
                    src = S[n % 2][:, :]
                    if u % 5 == 2:
                        dst = prob[:, h:h + 2, KC_AT[2]:KC_AT[2] + 256]
                        src = src.rearrange("p (h n) -> p h n", h=2)
                    else:
                        h, at = (h + u % 5 // 3, 0 if u % 5 in (0, 3) else 512)
                        dst = prob[:, h, at:at + 512]
                    act.activation(dst, src, ACT.Exp, scale=SCALE).then_inc(exp_done.sem, 1)

            def attended(b, g):
                act.wait_ge(pv_done.sem, pv_done.value(b, g + 1))
                if g:
                    act.wait_ge(a_ready.sem, a_filled(b, f"o{g - 1}"))
                act.activation(oT, OV[:, :], ACT.Copy).then_inc(oT_done.sem, 1)

            def iteration(b, late, older, nxt):
                for g in range(NG):
                    if b is not None:
                        exps(b, g, range(4))
                        if g:
                            attended(b, g - 1)
                        exps(b, g, range(4, SIMS_UNIT + 2))
                    if late is not None and g < 2:
                        similarities(late, 2 + g)
                    if b is not None:
                        exps(b, g, range(SIMS_UNIT + 2, UNITS))
                if b is not None:
                    attended(b, NG - 1)
                if nxt is not None:
                    act.wait_ge(c_ready.sem, c_filled(nxt, "xT"))
                    act.activation(xT[:, :], bank_c("xT")[:, :], ACT.Copy).then_inc(xT_done.sem, 1)
                    taken_qkv(nxt, 0)
                    taken_qkv(nxt, 1)
                if b is not None:
                    act.wait_ge(a_ready.sem, a_filled(b, "oTn"))
                    act.activation(oTn, A[:, :], ACT.Copy).then_inc(oTn_done.sem, 1)
                if late is not None:
                    act.activation(spare_out[:, 0:1], spare_in[:, :], ACT.Gelu)
                if nxt is not None:
                    first_parts(nxt, 0)
                    taken_qkv(nxt, 2)
                    taken_qkv(nxt, 3)
                if late is not None:
                    hidden(late, 0)
                    hidden(late, 1)
                if nxt is not None:
                    second_parts(nxt, 0)
                if late is not None:
                    for c in range(2, NHI):
                        hidden(late, c)
                if nxt is not None:
                    transposed(nxt, 0)
                    transposed(nxt, 1)
                if b is not None:
                    normed(b)
                if nxt is not None:
                    first_parts(nxt, 1)
                if b is not None:
                    similarities(b, 0)
                if nxt is not None:
                    second_parts(nxt, 1)
                if b is not None:
                    similarities(b, 1)
                if nxt is not None:
                    act.activation(spare_out[:, 1:2], spare_in[:, :], ACT.Exp)
                    transposed(nxt, 2)
                    transposed(nxt, 3)

            iteration(None, None, None, 0)
            iteration(0, None, None, 1)
            iteration(1, 0, None, 2)
            with act.Fori(2, BATCH - 1) as b:
                iteration(b, b - 1, b - 2, b + 1)
            iteration(BATCH - 1, BATCH - 2, BATCH - 3, None)
            iteration(None, BATCH - 1, BATCH - 2, None)
            iteration(None, None, BATCH - 1, None)

        @block.tensor
        def _(pe):
            pe.wait_ge(w_loaded, 160)
            pe.wait_ge(const_done, 4)
            raw = ([wqkv_raw[:, g, :] for g in range(3)] + [wproj_raw] + [down_raw[:, g, :] for g in range(8)]
                   + [keys_raw[:, c, s, :] for s in range(2) for c in range(2)])
            for bank, quad in zip((S[0], S[1], OV, A), range(4)):
                for i in range(4):
                    last = nc.tensor.transpose(bank[:, i * P:(i + 1) * P], raw[4 * quad + i], ident[:, :])
                last.then_inc(set_tr, 1)
            pe.wait_ge(set_ev, 4)
            for s in range(2):
                for h in range(H):
                    col = (s * H + h) * NK
                    last = nc.tensor.matmul(G[0][:, col:col + NK], wq_raw[:, 2 * h + s, :],
                                            keysT[:, col:col + NK], start=True, stop=True)
            last.then_inc(set_mm, 1)
            pe.wait_ge(set_w, 1)

            pe.wait_ge(bound_steps, 5)
            far_scores = pe.value_load(far[0:1, 0:1], min_val=0, max_val=1)

            def transpose_x(b):
                pe.wait_ge(xa_loaded.sem, xa_loaded.value(b, 16))
                wait_c_empty(pe, b, "xT")
                for t in range(NT):
                    last = nc.tensor.transpose(bank_c("xT")[:, t * P:(t + 1) * P], xa[:, t, :], ident[:, :])
                last.then_inc(c_ready.sem, 1)

            def project_qkv(b, t):
                if t == 0:
                    pe.wait_ge(xT_done.sem, xT_done.value(b, 1))
                wait_c_empty(pe, b, f"qkv{t}")
                nc.tensor.matmul(bank_c(f"qkv{t}")[:, 0:3 * D], xT[:, t * P:(t + 1) * P], wqkvT[:, :], start=True, stop=True)\
                    .then_inc(c_ready.sem, 1)

            def transpose_stack(b, t):
                pe.wait_ge(stack_done.sem, stack_done.value(b, t // 2 + 1))
                for side, use in enumerate("QK"):
                    wait_c_empty(pe, b, f"{use}{t}")
                    st = stack[:, side, t % 2].rearrange("p (j h) s d -> p j (h s d)", h=2)
                    for j in range(NPAIR):
                        last = nc.tensor.transpose(stacked(bank_c(f"{use}{t}"))[:, j, :], st[:, j, :], ident_b[:, :])
                    last.then_inc(c_ready.sem, 1)

            def shift_by_maxima(b):
                pe.wait_ge(kT_done.sem, kT_done.value(b, NT))
                wait_a_empty(pe, b, "o0")
                for t in range(NT):
                    keys_up_to = (t + 1) * P
                    for h in range(NH):
                        n = t * NH + h
                        if n:
                            pe.wait_ge(peak_done.sem, peak_done.value(b, n))
                        nc.tensor.matmul(A[:, 0:keys_up_to], qT[:, h // 2, t * P:keys_up_to],
                                         kT[h % 2][:, h // 2, 0:keys_up_to], start=True, stop=False,
                                         skip_group_check=True)
                        nc.tensor.matmul(A[:, t * P:keys_up_to], causal[:, :], ident_b[:, :], start=False,
                                         stop=True, skip_group_check=True).then_inc(peak_ready.sem, 1)
                pe.wait_ge(peak_done.sem, peak_done.value(b, NT * NH))
                for t in range(NT):
                    pe.wait_ge(shift_steps.sem, shift_steps.value(b, 1 + 4 * (t + 1)))
                    if t:
                        pe.wait_ge(shift_added.sem, shift_added.value(b, t))
                    st = shift.rearrange("p (j h) c d -> p j (h c d)", h=2)
                    for j in range(NPAIR):
                        last = nc.tensor.transpose(stacked(A)[:, j, :], st[:, j, :], ident_b[:, :])
                    last.then_inc(shift_turned.sem, 1)
                pe.wait_ge(shift_added.sem, shift_added.value(b, NT))

            def scores(b, g, units):
                if g == 0:
                    pe.wait_ge(kT_done.sem, kT_done.value(b, NT))
                for u in units:
                    n = g * UNITS + u
                    pe.wait_ge(exp_done.sem, exp_done.value(b, n - 1))
                    j = 2 * g + u // 5
                    bank = S[n % 2]
                    for half, kc, col in SCORES[u % 5]:
                        pe_k = kT[half][:, j, kc * P:(kc + 1) * P]
                        nc.tensor.matmul(bank[:, col:col + T - kc * P], pe_k, qT[:, j, kc * P:T],
                                         start=True, stop=False, skip_group_check=True)
                        last = nc.tensor.matmul(bank[:, col:col + P], ident_b[:, :], causal[:, :],
                                                start=False, stop=True, skip_group_check=True)
                    last.then_inc(s_ready.sem, 1)

            def attend(b, g):
                pe.wait_ge(exp_done.sem, exp_done.value(b, (g + 1) * UNITS))
                pe.wait_ge(oT_done.sem, oT_done.value(b, g))
                if g == 0:
                    pe.wait_ge(ln2.sem, ln2.value(b, 1 - 3 * ln2.per_batch))
                for kc in range(NT):
                    for i in range(4):
                        last = nc.tensor.matmul(
                            OV[32 * i:32 * i + HD + 1, kc * P:T], vp[:, kc, 4 * g + i, :],
                            prob[:, i, KC_AT[kc]:KC_AT[kc] + T - kc * P], start=(kc == 0), stop=(kc == NT - 1),
                            skip_group_check=True)
                last.then_inc(pv_done.sem, 1)

            def transpose_o(b, g):
                pe.wait_ge(oT_done.sem, oT_done.value(b, g + 1))
                wait_a_empty(pe, b, f"o{g}")
                for t in range(NT):
                    last = nc.tensor.transpose(A[:, t * P:(t + 1) * P], oT[:, t * P:(t + 1) * P], ident[:, :])
                last.then_inc(a_ready.sem, 1)

            def turn_outputs(b):
                pe.wait_ge(o_done.sem, o_done.value(b, NG))
                wait_a_empty(pe, b, "oTn")
                for t in range(NT):
                    last = nc.tensor.transpose(A[:, t * P:(t + 1) * P],
                                               o[:, t].rearrange("p h d -> p (h d)"), ident[:, :])
                last.then_inc(a_ready.sem, 1)

            def project_out(b):
                pe.wait_ge(oTn_done.sem, oTn_done.value(b, 1))
                wait_a_empty(pe, b, "proj")
                for t in range(NT):
                    last = nc.tensor.matmul(A[:, t * P:(t + 1) * P], oTn[:, t * P:(t + 1) * P], wprojT[:, :],
                                            start=True, stop=True)
                last.then_inc(a_ready.sem, 1)

            def project_similarities(b, t):
                bank = bank_f(f"sims{t}")
                wait_f_empty(pe, b, f"sims{t}")
                pe.wait_ge(xn_done.sem, xn_done.value(b, 1))
                nc.tensor.matmul(bank[:, :], xn[:, t * P:(t + 1) * P],
                                 simW[:, :, :, :].rearrange("p s h k -> p (s h k)"), start=True, stop=True)\
                    .then_inc(f_ready.sem, 1)

            def transpose_yi(b):
                bank = bank_f("xn")
                pe.wait_ge(yi_done.sem, yi_done.value(b, 1))
                wait_f_empty(pe, b, "xn")
                for t in range(NT):
                    last = nc.tensor.transpose(bank[:, t * P:(t + 1) * P], yi[:, t, :], ident[:, :])
                last.then_inc(f_ready.sem, 1)

            def hidden_products(b):
                for c in range(NHI):
                    bank = bank_f(f"hid{c}")
                    wait_f_empty(pe, b, f"hid{c}")
                    nc.tensor.matmul(bank[:, :], downT[:, c * P:(c + 1) * P], xn[:, :], start=True, stop=True)\
                        .then_inc(f_ready.sem, 1)

            def transpose_selection(b):
                bank = bank_f("sel")
                pe.wait_ge(esel_done.sem, esel_done.value(b, NT))
                wait_f_empty(pe, b, "sel")
                for pair in range(2):
                    two = slice(2 * pair, 2 * pair + 2)
                    nc.tensor.transpose(bank[:, pair * P:(pair + 1) * P],
                                        esel[:, two, :].rearrange("p t k -> p (t k)"), ident[:, :])
                    last = nc.tensor.transpose(bank[:, (2 + pair) * P:(3 + pair) * P],
                                               fsel[:, two].rearrange("p t h k -> p (t h k)"), ident[:, :])
                last.then_inc(f_ready.sem, 1)

            def weights(b, part):
                chunk, quarter = part // 4, part % 4
                pair, bank = chunk // 4, G[chunk % 2]
                if part % 16 == 0:
                    pe.wait_ge(hot_done.sem, hot_done.value(b, 2 + pair))
                if quarter == 0:
                    pe.wait_ge(g_free.sem, g_free.value(b, chunk - 1))
                for i in range(8 * quarter, 8 * quarter + 8):
                    t = chunk % 4 * 32 + i
                    for w_part in range(3):
                        last = nc.tensor.matmul(bank[:, 16 * i:16 * i + 16], onehot[:, :, pair, t],
                                                whot[:, w_part, :, :, t],
                                                start=(w_part == 0), stop=(w_part == 2))
                if quarter == 3:
                    last.then_inc(g_ready.sem, 1)

            def expert_outputs(b):
                pe.wait_ge(g_free.sem, g_free.value(b, 8))
                batches = min(3, BATCH - b) if isinstance(b, int) else 3
                pe.wait_ge(oT_done.sem, oT_done.value(b, NG * batches))
                for t in range(NT):
                    for c in range(NHI):
                        last = nc.tensor.matmul(OV[:, t * P:(t + 1) * P], hid[:, c, t * P:(t + 1) * P],
                                                up[:, c, :], start=(c == 0), stop=(c == NHI - 1))
                last.then_inc(ffn_ready.sem, 1)

            def iteration(b, late, older, nxt):
                for step in range(NG * UNITS):
                    g, u = step // UNITS, step % UNITS
                    if b is not None:
                        scores(b, g, [u])
                        if u == 1 and g:
                            attend(b, g - 1)
                    if older is not None and step in WEIGHT_STEPS:
                        weights(older, 8 + WEIGHT_STEPS.index(step))
                    if b is not None and u == UNITS - 1 and g:
                        transpose_o(b, g - 1)
                    if late is not None and u == SIMS_UNIT and g < 2:
                        project_similarities(late, 2 + g)
                    if late is not None and step == SELECTION_STEP:
                        transpose_selection(late)
                if b is not None:
                    attend(b, NG - 1)
                if nxt is not None:
                    transpose_x(nxt)
                if b is not None:
                    transpose_o(b, NG - 1)
                if nxt is not None:
                    project_qkv(nxt, 0)
                    project_qkv(nxt, 1)
                if b is not None:
                    turn_outputs(b)
                    project_out(b)
                if nxt is not None:
                    project_qkv(nxt, 2)
                    project_qkv(nxt, 3)
                if older is not None:
                    expert_outputs(older)
                if late is not None:
                    hidden_products(late)
                if nxt is not None:
                    transpose_stack(nxt, 0)
                    transpose_stack(nxt, 1)
                if b is not None:
                    transpose_yi(b)
                    project_similarities(b, 0)
                    project_similarities(b, 1)
                if nxt is not None:
                    transpose_stack(nxt, 2)
                if late is not None:
                    for part in range(0, 4):
                        weights(late, part)
                if nxt is not None:
                    transpose_stack(nxt, 3)
                if late is not None:
                    for part in range(4, 8):
                        weights(late, part)
                if nxt is not None:
                    with pe.If(far_scores != 0):
                        shift_by_maxima(nxt)

            iteration(None, None, None, 0)
            iteration(0, None, None, 1)
            iteration(1, 0, None, 2)
            with pe.Fori(2, BATCH - 1) as b:
                iteration(b, b - 1, b - 2, b + 1)
            iteration(BATCH - 1, BATCH - 2, BATCH - 3, None)
            iteration(None, BATCH - 1, BATCH - 2, None)
            iteration(None, None, BATCH - 1, None)

        @block.vector
        def _(dve):
            for s in seeded:
                dve.sem_inc(s.sem, s.seed)
            spare = (SLOTS - 2) * HD
            rows = stack[:, :, :, :, :, :].rearrange("p s t h c d -> p s (t h) (c d)")
            dve.memset(rows[:, 0, :, spare:], 0.0)
            dve.memset(rows[:, 1, :, spare + 3:], 0.0)
            dve.memset(rows[:, 1, :, spare:spare + 3], 1.0)
            dve.memset(kT[0][64:128, :, :], 0.0)
            dve.memset(kT[1][0:64, :, :], 0.0)
            dve.memset(whot[:, :, :, :, :], 0.0)
            dve.memset(vp[:, :, :, HD:HD + 1], 1.0)
            dve.wait_ge(w_loaded, 160)
            for tab, k in ((cosw, 0), (sinw, 1)):
                for s in range(2):
                    for half in range(2):
                        dve.scalar_tensor_tensor(
                            tab[:, :, s, 4 * half:4 * half + 4], rope[:, :, k, :], float(HD) ** 0.5,
                            qkw[:, s, 4 * half:4 * half + 4].unsqueeze(1).to_broadcast([P, NT, 4]),
                            ALU.mult, ALU.mult)
            dve.tensor_tensor(qkw_sq, qkw, qkw, ALU.mult).then_inc(bound_steps, 1)
            dve.wait_ge(bound_steps, 1)
            dve.tensor_tensor(pair_sq, qkw_sq[:, :, 0:4], qkw_sq[:, :, 4:8], ALU.max).then_inc(bound_steps, 1)
            dve.wait_ge(bound_steps, 2)
            dve.tensor_tensor(score_sq, pair_sq[:, 0, :], pair_sq[:, 1, :], ALU.mult).then_inc(bound_steps, 1)
            dve.wait_ge(bound_steps, 3)
            dve.tensor_reduce(most_sq, score_sq, AX.X, ALU.max).then_inc(bound_steps, 1)
            dve.wait_ge(bound_steps, 4)
            dve.tensor_scalar(far[:, :], most_sq, (SAFE_SCORE / (SCALE * HD)) ** 2, None, ALU.is_gt)\
                .then_inc(bound_steps, 1)
            dve.wait_ge(bound_steps, 5)
            far_scores = dve.value_load(far[0:1, 0:1], min_val=0, max_val=1)
            dve.wait_ge(set_tr, 4)
            dve.tensor_copy(wqkvT[:, :], S[0][:, 0:3 * P])
            dve.tensor_copy(wprojT[:, :], S[0][:, 3 * P:4 * P]).then_inc(set_ev, 1)
            dve.tensor_copy(downT[:, 0:512], S[1][:, :]).then_inc(set_ev, 1)
            dve.tensor_copy(downT[:, 512:1024], OV[:, :]).then_inc(set_ev, 1)
            dve.tensor_copy(keysT, A[:, :]).then_inc(set_ev, 1)
            dve.wait_ge(set_mm, 1)
            dve.tensor_copy(simW[:, :, :, :].rearrange("p s h k -> p (s h k)"), G[0][:, :]).then_inc(set_w, 1)

            def inverse_root(x, y, t, steps, b, n, beside=()):
                los = iter(beside)

                def step(instruction):
                    instruction.then_inc(steps.sem, 1)
                    for lo in islice(los, 1):
                        one_hot(lo)

                yb = y.bitcast(i32)
                step(dve.tensor_scalar(yb, x.bitcast(i32), 1, None, ALU.logical_shift_right))
                dve.wait_ge(steps.sem, steps.value(b, n + 1))
                step(dve.tensor_scalar(yb, yb, -1.0, float(0x5F3759DF), ALU.mult, ALU.add))
                for k in range(n + 2, n + ROOT_STEPS, 3):
                    dve.wait_ge(steps.sem, steps.value(b, k))
                    step(dve.tensor_tensor(t, x, y, ALU.mult))
                    dve.wait_ge(steps.sem, steps.value(b, k + 1))
                    step(dve.scalar_tensor_tensor(t, t, -0.5, y, ALU.mult, ALU.mult))
                    dve.wait_ge(steps.sem, steps.value(b, k + 2))
                    step(dve.scalar_tensor_tensor(y, t, 1.5, y, ALU.add, ALU.mult))
                dve.wait_ge(steps.sem, steps.value(b, n + ROOT_STEPS))

            def normalise(b, half, older=None, beside=()):
                n = half * (1 + ROOT_STEPS)
                groups = lambda a: a[:, :, :, :, :].rearrange("p s t h d -> p (s t h) d")
                dve.wait_ge(sq_done.sem, sq_done.value(b, 2 * half + 2))
                dve.tensor_reduce(qk_ms[:, 0:64], groups(qk_a), AX.X, ALU.add).then_inc(ms_done.sem, 1)
                dve.wait_ge(ms_done.sem, ms_done.value(b, half + 1))
                dve.tensor_scalar(qk_ms[:, 0:64], qk_ms[:, 0:64], HD * RMS_EPS, None, ALU.add)\
                    .then_inc(qroot.sem, 1)
                dve.wait_ge(qroot.sem, qroot.value(b, n + 1))
                cols = 64
                if older is not None:
                    dve.wait_ge(ln2.sem, ln2.value(older, 4))
                    cols = 64 + NT
                inverse_root(qk_ms[:, 0:cols], qk_rs[:, 0:cols], qk_t[:, 0:cols], qroot, b, n + 1, beside)
                dve.tensor_tensor(groups(qk_n), groups(qk_n), qk_rs[:, 0:64].unsqueeze(2).to_broadcast([P, 64, HD]),
                                  ALU.mult).then_inc(qn_done.sem, 1)

            def shift_by_maxima(b):
                for n in range(NT * NH):
                    t, h = n // NH, n % NH
                    dve.wait_ge(peak_ready.sem, peak_ready.value(b, n + 1))
                    dve.tensor_reduce(peak[:, t, h:h + 1], A[:, 0:(t + 1) * P], AX.X, ALU.max)\
                        .then_inc(peak_done.sem, 1)
                dve.wait_ge(peak_done.sem, peak_done.value(b, NT * NH))
                dve.wait_ge(stack_done.sem, stack_done.value(b, 2))
                dve.memset(shift, 0.0).then_inc(shift_steps.sem, 1)
                for t in range(NT):
                    dve.wait_ge(shift_steps.sem, shift_steps.value(b, 1 + 4 * t))
                    if t:
                        dve.wait_ge(shift_turned.sem, shift_turned.value(b, t))
                    first, second, third = (shift[:, :, SLOTS - 2, i] for i in range(3))
                    dve.tensor_scalar(first, peak[:, t, :], -1.0, None, ALU.mult).then_inc(shift_steps.sem, 1)
                    dve.wait_ge(shift_steps.sem, shift_steps.value(b, 2 + 4 * t))
                    dve.scalar_tensor_tensor(peak_rest[:, t, :], peak[:, t, :], -1.0, first, ALU.mult,
                                             ALU.subtract).then_inc(shift_steps.sem, 1)
                    dve.wait_ge(shift_steps.sem, shift_steps.value(b, 3 + 4 * t))
                    dve.tensor_copy(second, peak_rest[:, t, :]).then_inc(shift_steps.sem, 1)
                    dve.wait_ge(shift_steps.sem, shift_steps.value(b, 4 + 4 * t))
                    dve.tensor_tensor(third, peak_rest[:, t, :], second, ALU.subtract)\
                        .then_inc(shift_steps.sem, 1)
                    dve.wait_ge(shift_turned.sem, shift_turned.value(b, t + 1))
                    qt = qT[:, :, t * P:(t + 1) * P]
                    dve.tensor_tensor(qt, qt, stacked(A), ALU.add).then_inc(shift_added.sem, 1)

            def normalise_o(b, g):
                if g == 0:
                    dve.wait_ge(out_stored.sem, out_stored.value(b, -32))
                dve.wait_ge(a_ready.sem, a_filled(b, f"o{g}"))
                heads = A[:, :].rearrange("p (t h c) -> p t h c", t=NT, h=4)
                dve.reciprocal(rden[:, :, :], heads[:, :, :, HD]).then_inc(rden_done.sem, 1)
                dve.wait_ge(rden_done.sem, rden_done.value(b, g + 1))
                dve.tensor_tensor(o[:, :, 4 * g:4 * g + 4, :], heads[:, :, :, 0:HD],
                                  rden[:, :, :].unsqueeze(3).to_broadcast([P, NT, 4, HD]), ALU.mult)\
                    .then_inc(o_done.sem, 1)

            def moments(src, i, steps, b):
                dve.wait_ge(steps.sem, steps.value(b, 1))
                for t in range(NT):
                    last = dve.bn_stats(stats[:, t, :], src[:, t, :])
                last.then_inc(steps.sem, 1)
                dve.wait_ge(steps.sem, steps.value(b, 2))
                pass_wait(dve)
                for t in range(NT):
                    last = dve.bn_aggr(mv[i][:, t, :], stats[:, t, :])
                last.then_inc(steps.sem, 1)
                dve.wait_ge(steps.sem, steps.value(b, 3))

            def norm1(b, beside=()):
                dve.wait_ge(a_ready.sem, a_filled(b, "proj"))
                dve.wait_ge(xr_loaded.sem, xr_loaded.value(b, 16))
                dve.tensor_tensor(r1[:, :, :].rearrange("p t d -> p (t d)"), A[:, :],
                                  xr[:, :, :].rearrange("p t d -> p (t d)"), ALU.add).then_inc(ln1.sem, 1)
                moments(r1, 0, ln1, b)
                dve.tensor_scalar(var[:, 0, :], mv[0][:, :, 1], LN_EPS, None, ALU.add)
                dve.tensor_scalar(var[:, 1, :], mv[0][:, :, 1], 1.0 + RMS_EPS, RMS_EPS * LN_EPS,
                                  ALU.mult, ALU.add).then_inc(ln1.sem, 1)
                dve.wait_ge(ln1.sem, ln1.value(b, 4))
                inverse_root(var[:, :, :], rs[:, :, :], rs_t[:, :, :], ln1, b, 4, beside)
                for t in range(NT):
                    last = dve.tensor_scalar(yi[:, t, :], r1[:, t, :], mv[0][:, t, 0:1], rs[:, 1, t:t + 1],
                                             ALU.subtract, ALU.mult)
                last.then_inc(yi_done.sem, 1)

            def norm1_rows(b):
                dve.wait_ge(kept.sem, kept.value(b, 0))
                for t in range(NT):
                    last = dve.tensor_scalar(y_new[:, t, :], r1[:, t, :], mv[0][:, t, 0:1], rs[:, 0, t:t + 1],
                                             ALU.subtract, ALU.mult)
                last.then_inc(ln1.sem, 1)

            def norm2(b):
                dve.wait_ge(ffn_ready.sem, ffn_ready.value(b, 1))
                dve.wait_ge(out_stored.sem, out_stored.value(b, 0))
                dve.wait_ge(kept.sem, kept.value(b, 1))
                dve.tensor_tensor(r2[:, :, :].rearrange("p t d -> p (t d)"), OV[:, :],
                                  y[:, :, :].rearrange("p t d -> p (t d)"), ALU.add).then_inc(ln2.sem, 1)
                moments(r2, 1, ln2, b)
                dve.tensor_scalar(qk_ms[:, 64:64 + NT], mv[1][:, :, 1], LN_EPS, None, ALU.add)\
                    .then_inc(ln2.sem, 1)

            def norm2_root(b):
                dve.wait_ge(ln2.sem, ln2.value(b, 4))
                inverse_root(qk_ms[:, 64:64 + NT], qk_rs[:, 64:64 + NT], qk_t[:, 64:64 + NT], root_alone,
                             b - (BATCH - 3), 0)

            def norm2_rows(b):
                for t in range(NT):
                    last = dve.tensor_scalar(r2[:, t, :], r2[:, t, :], mv[1][:, t, 0:1],
                                             qk_rs[:, 64 + t:65 + t], ALU.subtract, ALU.mult)
                last.then_inc(out_ready.sem, 1)

            def top_keys(b, t):
                dve.wait_ge(sims_done.sem, sims_done.value(b, t + 1))
                pass_wait(dve)
                for s in range(2):
                    for h in range(H):
                        last = dve.max(out=topv[:, t, s, h, :], in_=sims[:, t % 2, s, h, :])
                last.then_inc(topv_done.sem, 1)
                dve.wait_ge(topv_done.sem, topv_done.value(b, t + 1))
                pass_wait(dve)
                for s in range(2):
                    for h in range(H):
                        last = dve.max_index(topi[:, t, s, h, :], topv[:, t, s, h, :], sims[:, t % 2, s, h, :])
                last.then_inc(top1_done.sem, 1)

            def top_pairs(b, t):
                if t == 0 and not (isinstance(b, int) and b + 1 >= BATCH):
                    dve.wait_ge(stack_done.sem, stack_done.value(b + 1, 2))
                dve.wait_ge(cand_done.sem, cand_done.value(b, t + 1))
                pass_wait(dve)
                for h in range(H):
                    last = dve.max(out=fsel[:, t, h, :], in_=candv[:, t % 2, h, :])
                last.then_inc(fsel_done.sem, 1)
                dve.wait_ge(fsel_done.sem, fsel_done.value(b, t + 1))
                pass_wait(dve)
                for h in range(H):
                    last = dve.max_index(psel[:, t % 2, h, :], fsel[:, t, h, :], candv[:, t % 2, h, :])
                last.then_inc(top2_done.sem, 1)
                dve.wait_ge(top2_done.sem, top2_done.value(b, t + 1))
                dims = [P, H, NCAND, TOPK]
                dve.tensor_tensor(gat[:, t % 2], psel[:, t % 2].unsqueeze(2).to_broadcast(dims),
                                  cand_no[:, :, :].unsqueeze(1).to_broadcast(dims), ALU.is_equal)\
                    .then_inc(hotc_done.sem, 1)

            def selected(b, t):
                dve.wait_ge(gat_done.sem, gat_done.value(b, 2 * t + 2))
                dve.tensor_reduce(esel[:, t, :].rearrange("p (h k) -> p h k", h=H),
                                  gat[:, t % 2, :, 0:10, :].rearrange("p h c k -> p h k c"), AX.X, ALU.add).then_inc(esel_done.sem, 1)

            def decode(b):
                bank = bank_f("sel")
                flat = lambda a: a.rearrange("p a t -> p (a t)")
                e, w = bank[:, 0:2 * P], bank[:, 2 * P:4 * P]
                w0, w1, w2 = (flat(wpart[:, i]) for i in range(3))
                dve.wait_ge(f_ready.sem, f_filled(b, "sel"))
                dve.tensor_copy(flat(eint[:, :, :]), e)
                dve.tensor_scalar(w0, w, 0.0, None, ALU.max).then_inc(dec.sem, 1)
                dve.wait_ge(dec.sem, dec.value(b, 1))
                dve.tensor_scalar(flat(elo[:, :, :]), flat(eint[:, :, :]), P - 1, None, ALU.bitwise_and)
                dve.tensor_scalar(flat(ehi[:, :, :]), flat(eint[:, :, :]), NEXP - P, None, ALU.bitwise_and)
                dve.scalar_tensor_tensor(flat(wrest[:, :, :]), w, 0.0, w0, ALU.max, ALU.subtract)\
                    .then_inc(dec.sem, 1)
                dve.wait_ge(dec.sem, dec.value(b, 2))
                dve.tensor_copy(w1, flat(wrest[:, :, :])).then_inc(dec.sem, 1)
                dve.wait_ge(dec.sem, dec.value(b, 3))
                dve.tensor_tensor(w2, flat(wrest[:, :, :]), w1, ALU.subtract).then_inc(dec.sem, 1)

            def one_hot(lo):
                dve.tensor_scalar(onehot[:, lo, :, :], elo[:, :, :], float(lo), None, ALU.is_equal)

            def one_hots(los):
                for lo in los:
                    one_hot(lo)

            def hi_one_hots(b):
                for hi in range(NHI):
                    last = dve.tensor_scalar(hot_hi[:, hi, :], ehi[:, :, :].rearrange("p a t -> p (a t)"),
                                             float(hi * P), None, ALU.is_equal)
                last.then_inc(hot_done.sem, 1)

            def weighted_one_hots(b, pair):
                dve.wait_ge(dec.sem, dec.value(b, 4))
                dve.wait_ge(hot_done.sem, hot_done.value(b, 1))
                if pair == 1:
                    dve.wait_ge(g_ready.sem, g_ready.value(b, 4))
                for part in range(3):
                    for i in range(2):
                        rows = slice(64 * i, 64 * i + 64)
                        w = wpart[rows, part, pair, :].unsqueeze(1).to_broadcast([64, NHI, P])
                        last = dve.tensor_tensor(whot[rows, part, i], hot_hi[rows, :, pair * P:pair * P + P], w,
                                                 ALU.mult)
                last.then_inc(hot_done.sem, 1)

            def apply_weights(b, chunk):
                if chunk == 0:
                    dve.wait_ge(hid_done.sem, hid_done.value(b, NHI))
                dve.wait_ge(g_ready.sem, g_ready.value(b, chunk + 1))
                pair, t0 = chunk // 4, chunk % 4 * 32
                h = hid[:, :, :].rearrange("p c (a s t) -> p a s c t", a=2, s=2)[:, pair, :, :, t0:t0 + 32]
                g = G[chunk % 2][:, :].rearrange("p (t s c) -> p s c t", s=2, c=NHI)
                dve.tensor_tensor(h, g, h, ALU.mult).then_inc(g_free.sem, 1)

            def iteration(b, late, older, oldest, nxt):
                if oldest is not None:
                    norm2_rows(oldest)
                if late is not None:
                    norm1_rows(late)
                if older is not None:
                    apply_weights(older, 2)
                if late is not None:
                    top_pairs(late, 0)
                    top_keys(late, 2)
                if older is not None:
                    apply_weights(older, 3)
                    weighted_one_hots(older, 1)
                if late is not None:
                    top_pairs(late, 1)
                    selected(late, 0)
                    top_keys(late, 3)
                if b is not None:
                    normalise_o(b, 0)
                if older is not None:
                    apply_weights(older, 4)
                if late is not None:
                    top_pairs(late, 2)
                    selected(late, 1)
                if older is not None:
                    apply_weights(older, 5)
                if late is not None:
                    top_pairs(late, 3)
                    selected(late, 2)
                if b is not None:
                    normalise_o(b, 1)
                if older is not None:
                    apply_weights(older, 6)
                if late is not None:
                    selected(late, 3)
                if older is not None:
                    apply_weights(older, 7)
                if late is not None:
                    decode(late)
                hot = (lambda first, last: range(first, last)) if late is not None else (lambda first, last: ())
                one_hots(hot(0, 20))
                if b is not None:
                    normalise_o(b, 2)
                one_hots(hot(20, 34))
                if b is not None:
                    normalise_o(b, 3)
                one_hots(hot(34, 46))
                if nxt is not None:
                    normalise(nxt, 0, beside=hot(46, 56))
                else:
                    one_hots(hot(46, 56))
                if b is not None:
                    norm1(b, beside=hot(56, 66))
                else:
                    one_hots(hot(56, 66))
                one_hots(hot(66, 72))
                if older is not None:
                    norm2(older)
                if nxt is not None:
                    normalise(nxt, 1, older, beside=hot(72, 82))
                else:
                    one_hots(hot(72, 82))
                    if older is not None:
                        norm2_root(older)
                one_hots(hot(82, P))
                if late is not None:
                    hi_one_hots(late)
                    weighted_one_hots(late, 0)
                if b is not None:
                    top_keys(b, 0)
                if late is not None:
                    apply_weights(late, 0)
                if b is not None:
                    top_keys(b, 1)
                if late is not None:
                    apply_weights(late, 1)
                if nxt is not None:
                    with dve.If(far_scores != 0):
                        shift_by_maxima(nxt)

            iteration(None, None, None, None, 0)
            iteration(0, None, None, None, 1)
            iteration(1, 0, None, None, 2)
            iteration(2, 1, 0, None, 3)
            with dve.Fori(3, BATCH - 1) as b:
                iteration(b, b - 1, b - 2, b - 3, b + 1)
            iteration(BATCH - 1, BATCH - 2, BATCH - 3, BATCH - 4, None)
            iteration(None, BATCH - 1, BATCH - 2, BATCH - 3, None)
            iteration(None, None, BATCH - 1, BATCH - 2, None)
            norm2_rows(BATCH - 1)


_INS = ["L0_attn_x", "L0_attn_w_qkv", "L0_attn_w_proj", "L0_attn_q_norm_w", "L0_attn_k_norm_w", "L0_ffn_w_q",
        "L0_ffn_keys", "L0_ffn_expert_down", "L0_ffn_expert_up", "L0_ffn_norm_w"]


def rope_constants(seq_len, head_dim, theta):
    import numpy as np
    freqs = theta ** (-np.arange(0, head_dim, 2, dtype=np.float32) / head_dim)
    ang = np.arange(seq_len, dtype=np.float32)[:, None] * freqs.astype(np.float32)[None, :]
    return np.stack([np.cos(ang), np.sin(ang)], axis=1).astype(np.float32)


def kernel(**inputs):
    import numpy as np
    import concourse.bacc as bacc
    from concourse import mybir
    from concourse.bass_utils import run_bass_kernel_spmd

    nc = bacc.Bacc("TRN2", target_bir_lowering=False, num_devices=1)
    arrays = {f"in_{n}": np.ascontiguousarray(inputs[n]) for n in _INS}
    arrays["in_rope"] = rope_constants(inputs["L0_attn_x"].shape[1], inputs["L0_attn_q_norm_w"].shape[0], 32.0)
    args = [nc.dram_tensor(n, a.shape, mybir.dt.from_np(a.dtype), kind="ExternalInput").ap()
            for n, a in arrays.items()]
    out = nc.dram_tensor("out", inputs["L0_attn_x"].shape, mybir.dt.float32, kind="ExternalOutput").ap()
    attention_then_peer_layer(nc, *args, out)
    return run_bass_kernel_spmd(nc, [arrays], core_ids=[0]).results[0]["out"]
```
